# Optimizing a Trainium2 kernel written in Bass

```python
import numpy as np
import jax
import jax.numpy as jnp

def _softmax(x, axis=-1):
    return jax.nn.softmax(x, axis=axis)

def _gelu(x):
    return jax.nn.gelu(x, approximate=True)

def _silu(x):
    return jax.nn.silu(x)

def _sigmoid(x):
    return jax.nn.sigmoid(x)

def _layernorm(x, axis=-1, eps=1e-05):
    m = jnp.mean(x, axis=axis, keepdims=True)
    v = jnp.var(x, axis=axis, keepdims=True)
    return (x - m) / jnp.sqrt(v + eps)

def _scatter_add(tgt, idx, src, axis=0):
    return tgt.at[idx].add(src)

def _segment_sum(src, seg, n):
    return jax.ops.segment_sum(src, seg, n)
kernel_name = 'mk_gnn_resnorm_d1_gnn_r8_d344b7'

def setup_inputs(seed: int=0):
    np.random.seed(seed)
    _w = jnp.asarray

    def _rec_inputs():
        import jax
        import jax.numpy as jnp
        _gk = jax.random.key(seed)
        x = -0.000202 + 1 * jax.random.normal(jax.random.fold_in(_gk, 1), (6250, 128), jnp.float32)
        _s = jax.random.randint(jax.random.fold_in(_gk, 2), (50000,), 0, 6250, jnp.int32)
        _d = jax.random.randint(jax.random.fold_in(_gk, 3), (50000,), 0, 6250, jnp.int32)
        _loop = jnp.arange(6250, dtype=jnp.int32)
        src = jnp.concatenate([_s, _d, _loop])
        dst = jnp.concatenate([_d, _s, _loop])
        _o = jnp.argsort(dst, stable=True)
        src = src[_o]
        dst = dst[_o]
        edge_attr_128 = -6.74381e-05 + 0.999835 * jax.random.normal(jax.random.fold_in(_gk, 12), (106250, 128), jnp.float32)
        return (x, src, dst, edge_attr_128)
    x, src, dst, edge_attr_128 = _rec_inputs()

    def _L0_gnn_setup():
        import jax, jax.numpy as jnp
        import numpy as np
        N, E, D, L = (6250, 78125, 128, 2)
        NEG_SLOPE = 0.01

        def _segment_softmax(e, seg, num_segments):
            m = jax.ops.segment_max(e, seg, num_segments=num_segments)
            ex = jnp.exp(e - m[seg])
            s = jax.ops.segment_sum(ex, seg, num_segments=num_segments)
            return ex / s[seg]
        key = jax.random.key(seed)
        ks = jax.random.split(key, 8)
        s = 1.0 / np.sqrt(D)
        return {'x': jax.random.normal(ks[0], (N, D), jnp.float32), 'r_h': jax.random.normal(ks[1], (E, D), jnp.float32), 'src': jax.random.randint(ks[2], (E,), 0, N), 'dst': jax.random.randint(ks[3], (E,), 0, N), 'W': jax.random.normal(ks[4], (L, D, D), jnp.float32) * s, 'Wr': jax.random.normal(ks[5], (L, D, D), jnp.float32) * s, 'Att': jax.random.normal(ks[6], (L, 3 * D), jnp.float32) * s, 'Loop': jax.random.normal(ks[7], (L, D, D), jnp.float32) * s}
    _L0_gnn_all = _L0_gnn_setup()
    _L0_gnn_in = {k: v for k, v in _L0_gnn_all.items() if k in ('W', 'Wr', 'Att', 'Loop')}
    del _L0_gnn_all
    return {'x': x, 'src': src, 'dst': dst, 'edge_attr_128': edge_attr_128, 'L0_gnn_W': _L0_gnn_in['W'], 'L0_gnn_Wr': _L0_gnn_in['Wr'], 'L0_gnn_Att': _L0_gnn_in['Att'], 'L0_gnn_Loop': _L0_gnn_in['Loop']}

def reference(x, src, dst, edge_attr_128, L0_gnn_W, L0_gnn_Wr, L0_gnn_Att, L0_gnn_Loop):
    import jax
    import jax.numpy as jnp

    def _L0_gnn_ref(x, r_h, src, dst, W, Wr, Att, Loop):
        import jax, jax.numpy as jnp
        import numpy as np
        N, E, D, L = (6250, 78125, 128, 2)
        NEG_SLOPE = 0.01

        def _segment_softmax(e, seg, num_segments):
            m = jax.ops.segment_max(e, seg, num_segments=num_segments)
            ex = jnp.exp(e - m[seg])
            s = jax.ops.segment_sum(ex, seg, num_segments=num_segments)
            return ex / s[seg]
        n = x.shape[0]
        h = x
        for l in range(W.shape[0]):
            hh = h @ W[l]
            rh = r_h @ Wr[l]
            hs = hh[src]
            a = Att[l]
            d = hh.shape[1]
            e = hs @ a[:d] + (hh @ a[d:2 * d])[dst] + rh @ a[2 * d:]
            e = jnp.where(e > 0, e, NEG_SLOPE * e)
            alpha = _segment_softmax(e, dst, n)
            msg = alpha[:, None] * (hs + rh)
            agg = jax.ops.segment_sum(msg, dst, num_segments=n)
            h = jax.nn.relu(agg + hh @ Loop[l])
        return h
    x = _layernorm(x + _L0_gnn_ref(x, edge_attr_128, src, dst, L0_gnn_W, L0_gnn_Wr, L0_gnn_Att, L0_gnn_Loop), axis=-1)
    return x

_drawn_inputs = setup_inputs


def setup_inputs(seed=0):
    import zlib

    import numpy as np

    out = dict(_drawn_inputs(seed))
    spreads = {}
    factors = {}
    for name, (base, spread) in spreads.items():
        noise = np.random.default_rng([zlib.crc32(name.encode()), seed]).standard_normal(out[name].shape)
        drawn = base * np.exp(spread * noise) if base else spread * noise
        out[name] = jnp.asarray(drawn.astype(out[name].dtype))
    for name, factor in factors.items():
        out[name] = (out[name] * factor).astype(out[name].dtype)
    return out
```

```python
from contextlib import ExitStack

import concourse.bass as bass
from concourse import mybir


F32 = mybir.dt.float32
I32 = mybir.dt.int32
ALU = mybir.AluOpType
ACT = mybir.ActivationFunctionType
AX = mybir.AxisListType

P = 128
D = 128
K = 13
RING = 4
NEG_SLOPE = 0.01
EPS = 1e-5
BIG = 1e30
TINY = 1e-30

C_ONE = 2 * D
C_HOT = C_ONE + 1
C_ROW = C_HOT + P
C_PITCH = C_ROW + 3


def gnn_program(nc, x, src, dst, dst_flat, edge_attr, weights, rel_weights, att, loop_weights, out, plan):
    N, E, G, L = plan["nodes"], plan["edges"], plan["groups"], plan["layers"]
    GROUP = K * P
    HALF_A = K // 2
    TURNS = G // RING
    FULL_TILES = E // P
    TILES = -(-E // P)
    BLOCKS = N // P + 1
    DUMP = BLOCKS * P

    hidden = nc.dram_tensor("hidden", (N + P, D), F32, kind="Internal").ap()
    row_masks = nc.dram_tensor("row_masks", (G, 4 * P), F32, kind="Internal").ap()
    node_sums = nc.dram_tensor("node_sums", (DUMP + P, C_HOT + 1), F32, kind="Internal").ap()

    with ExitStack() as ctx:
        def sb(name, shape, dt=F32):
            return ctx.enter_context(nc.sbuf_tensor(name, shape, dt))

        def psum(name):
            return ctx.enter_context(nc.psum_tensor(name, [P, 512], F32))

        def sem(name):
            return ctx.enter_context(nc.semaphore(name))

        ones = sb("ones", [P, P])
        column = sb("column", [P, P])
        partition = sb("partition", [P, 1])
        identity = sb("identity", [P, P])
        shift_down = sb("shift_down", [P, P])
        shift_up = sb("shift_up", [P, P])
        last_to_first = sb("last_to_first", [P, P])
        from_first = sb("from_first", [P, P])
        from_last = sb("from_last", [P, P])
        minus_first = sb("minus_first", [P, P])
        eps = sb("eps", [P, 1])

        w_sb = sb("w_sb", [P, L, D])
        wr_sb = sb("wr_sb", [P, L, D])
        loop_sb = sb("loop_sb", [P, L, D])
        att_sb = sb("att_sb", [P, L * 3])
        w_turned = sb("w_turned", [P, L, D])
        wr_turned = sb("wr_turned", [P, L, D])
        w_loop = sb("w_loop", [P, L, D])
        att_wide = sb("att_wide", [P, L, 3, P])
        dst_wide = sb("dst_wide", [P, L, P])
        score_w = [[sb(f"score_w{l}{b}", [P, C_ROW]) for b in range(2)] for l in range(L)]

        dst_int = sb("dst_int", [P, G, K], I32)
        dst_f = sb("dst_f", [P, G, K])
        rel = sb("rel", [P, G, K])
        last_before = sb("last_before", [P, G])
        base = sb("base", [P, G])
        base_step = sb("base_step", [P, G])
        base_int = sb("base_int", [1, G], I32)
        carry_pen = sb("carry_pen", [P, G])
        step_pen = sb("step_pen", [P, G, K + 1])
        back_pen = sb("back_pen", [P, G, K])
        head_pen = sb("head_pen", [P, G, K])
        tail_pen = sb("tail_pen", [P, G, K])
        firsts_t = sb("firsts_t", [G, P])
        lasts_t = sb("lasts_t", [G, P])
        before_t = sb("before_t", [G, P])
        masks_t = sb("masks_t", [G, 4, P])
        spans_t = sb("spans_t", [G, P])
        unsorted = sb("unsorted", [P, G, K])
        wide = sb("wide", [P, G])
        faults = sb("faults", [P, 4])
        fault_row = sb("fault_row", [1, 1])
        general = sb("general", [1, 1], I32)

        rows = sb("rows", [P, RING, K, C_PITCH])
        products = sb("products", [P, K, C_ROW])
        src_idx = sb("src_idx", [P, RING, K], I32)
        mask_row = sb("mask_row", [1, RING, 4 * P])
        window = sb("window", [P, RING, D])
        residual = sb("residual", [P, RING, D])
        window_t = sb("window_t", [P, RING, D])
        score_raw = sb("score_raw", [P, 2, K])
        score = sb("score", [P, 2, K])
        run_fwd = sb("run_fwd", [P, 2, K])
        run_bwd = sb("run_bwd", [P, 2, K])
        carried = sb("carried", [1, 2, 2 * P])
        peak_a = sb("peak_a", [P, 2, K])
        peak_b = sb("peak_b", [P, 2, K])
        peak = sb("peak", [P, 2, K])
        lowered = sb("lowered", [P, 2, K])
        alpha = sb("alpha", [P, 2, K])
        drop = sb("drop", [P, 2])
        carry_m = [sb(f"carry_m{b}", [P, P]) for b in range(2)]
        weighted = sb("weighted", [P, 2, K, P])
        sums = [sb(f"sums{b}", [P, C_HOT]) for b in range(2)]
        total = sb("total", [P, 2])
        inv_total = sb("inv_total", [P, 2])
        mean_rows = sb("mean_rows", [P, 2 * D])
        mean_t = sb("mean_t", [P, 2 * D])
        result = [sb(f"result{b}", [P, D]) for b in range(2)]
        summed = [sb(f"summed{b}", [P, D]) for b in range(2)]
        stats = sb("stats", [P, 2, 6])
        mean_var = sb("mean_var", [P, 2, 2])
        log_var = sb("log_var", [P, 2])
        inv_std = sb("inv_std", [P, 2])

        tile_src = sb("tile_src", [P, 1], I32)
        tile_dst = sb("tile_dst", [P, 1], I32)
        tile_dst_f = sb("tile_dst_f", [P, 1])
        below = sb("below", [P, P])
        spread = sb("spread", [P, 2, P])
        other_pen = sb("other_pen", [P, P])
        same = sb("same", [P, P])
        masked = sb("masked", [P, P])
        tile_work = sb("tile_work", [P, 16])
        tile_rows = sb("tile_rows", [P, C_HOT])
        old_sums = sb("old_sums", [P, C_HOT + 1])
        new_sums = sb("new_sums", [P, C_HOT + 1])
        empty_sums = sb("empty_sums", [P, C_HOT + 1])
        sums_row = sb("sums_row", [P, 1], I32)

        ps_sum = [psum(f"ps_sum{b}") for b in range(2)]
        ps_win = [psum(f"ps_win{b}") for b in range(2)]
        ps_turn = psum("ps_turn")
        ps_out = psum("ps_out")
        ps_row = psum("ps_row")
        ps_col = psum("ps_col")

        dst_loaded = sem("dst_loaded")
        weights_loaded = sem("weights_loaded")
        pool_made = sem("pool_made")
        selectors = sem("selectors")
        dve_made = sem("dve_made")
        pe_made = sem("pe_made")
        masks_stored = sem("masks_stored")
        rows_loaded = [sem(f"rows_loaded{s}") for s in range(RING)]
        idx_loaded = [sem(f"idx_loaded{s}") for s in range(RING)]
        mask_loaded = [sem(f"mask_loaded{s}") for s in range(RING)]
        window_loaded = [sem(f"window_loaded{s}") for s in range(RING)]
        residual_loaded = [sem(f"residual_loaded{s}") for s in range(RING)]
        gathered = [sem(f"gathered{s}") for s in range(RING)]
        hot_made = sem("hot_made")
        window_turned = sem("window_turned")
        window_t_made = sem("window_t_made")
        dst_scored = sem("dst_scored")
        score_w_made = sem("score_w_made")
        raw_made = sem("raw_made")
        score_made = sem("score_made")
        runs_made = sem("runs_made")
        row_ready = sem("row_ready")
        carried_made = sem("carried_made")
        col_ready = sem("col_ready")
        peak_a_made = sem("peak_a_made")
        peak_b_made = sem("peak_b_made")
        peak_made = sem("peak_made")
        lowered_made = sem("lowered_made")
        drop_ready = sem("drop_ready")
        drop_made = sem("drop_made")
        alpha_made = sem("alpha_made")
        carry_made = sem("carry_made")
        weighted_made = sem("weighted_made")
        summed_up = sem("summed_up")
        total_made = sem("total_made")
        inv_total_made = sem("inv_total_made")
        sums_made = sem("sums_made")
        mean_made = sem("mean_made")
        mean_turned = sem("mean_turned")
        mean_t_made = sem("mean_t_made")
        out_ready = sem("out_ready")
        result_made = sem("result_made")
        summed_made = sem("summed_made")
        stats_made = sem("stats_made")
        mean_var_made = sem("mean_var_made")
        log_var_made = sem("log_var_made")
        inv_std_made = sem("inv_std_made")
        stored = sem("stored")
        general_ready = sem("general_ready")
        emptied = sem("emptied")
        tile_loaded = [sem(f"tile_loaded{l}") for l in range(L)]
        tile_gathered = [sem(f"tile_gathered{l}") for l in range(L)]
        tile_added = sem("tile_added")
        tile_step = sem("tile_step")
        block_loaded = sem("block_loaded")
        block_step = sem("block_step")
        block_stored = sem("block_stored")
        passed = sem("passed")

        block = ctx.enter_context(nc.Block())

        def node_table(l):
            return x if l == 0 else hidden

        def uses(l, turn):
            return l * TURNS + turn + 1

        def row_uses(l, turn, slot, short):
            extra = 1 if slot == (G - 1) % RING else 0
            return uses(l, turn) + l * extra + (extra if short else 0)

        TILE_STEPS = ("dst_float", "raw", "score", "spread_score", "spread_dst", "lay_out", "other_pen",
                      "same", "masked", "tile_peak", "new_peak", "lowered", "old_lowered", "repeats",
                      "alpha", "old_scale", "weigh", "add_up", "new_sums", "keep_peak", "is_repeat",
                      "dump_gap", "row_float", "row_int")
        BLOCK_STEPS = ("total", "inverse", "mean", "turn", "mean_turned", "window_turned", "product",
                       "relu", "stats", "aggregate", "log", "inv_std", "normalise")

        def tile_before(name, c):
            return len(TILE_STEPS) * (c - 1) + TILE_STEPS.index(name)

        def block_before(name, c):
            return len(BLOCK_STEPS) * (c - 1) + BLOCK_STEPS.index(name)

        def each_tile(eng, l, body):
            with eng.Fori(0, FULL_TILES) as tile:
                body(tile, l * TILES + tile + 1, False)
            if TILES > FULL_TILES:
                body(FULL_TILES, l * TILES + FULL_TILES + 1, True)

        def each_block(eng, l, body):
            with eng.Fori(0, BLOCKS) as blk:
                body(blk, l * BLOCKS + blk + 1)

        def by_path(eng, grouped, anything):
            eng.wait_ge(general_ready, 1)
            chosen = eng.value_load(general[0:1, 0:1], min_val=0, max_val=1)
            with eng.If(chosen > 0):
                anything()
            with eng.Else():
                grouped()

        def turns(eng, body):
            body(0, True, False)
            with eng.Fori(1, TURNS - 1) as turn:
                body(turn, False, False)
            body(TURNS - 1, False, True)

        DVE_ONES, DVE_DST = 8, 10
        DVE_TURNED = 17
        DVE_MASKS = 27
        DVE_ATT = 45
        DVE_ALL = 53

        SELECTORS = [(identity, 0, -1, 1.0), (shift_down, 1, -1, 1.0), (shift_up, -1, -1, 1.0),
                     (last_to_first, -(P - 1), P, 1.0), (from_first, 0, 0, 1.0),
                     (from_last, -(P - 1), 0, 1.0), (minus_first, 0, 0, -1.0)]

        @block.gpsimd
        def _(pool):
            for n, (tile, _, _, _) in enumerate(SELECTORS):
                nc.gpsimd.memset(tile[:], 0.0).then_inc(selectors, 1)
            pool.wait_ge(selectors, len(SELECTORS))
            for tile, first, step, value in SELECTORS:
                nc.gpsimd.affine_select(out=tile[:], in_=tile[:], compare_op=ALU.not_equal, fill=value,
                                        base=first, pattern=[[step, P]],
                                        channel_multiplier=1).then_inc(selectors, 1)
            nc.gpsimd.iota(column[:], [[1, P]], base=0, channel_multiplier=0,
                           allow_small_or_imprecise_dtypes=True).then_inc(selectors, 1)
            nc.gpsimd.iota(partition[:], [[0, 1]], base=0, channel_multiplier=1,
                           allow_small_or_imprecise_dtypes=True).then_inc(selectors, 1)

            def grouped():
                for l in range(L):
                    if l > 0:
                        pool.wait_ge(stored, 16 * G * l)
                    table = node_table(l)[0:N, :]

                    def body(turn, first, last):
                        for slot in range(RING):
                            n = l * G + RING * turn + slot + 1
                            if not (first and l == 0):
                                pool.wait_ge(summed_up, n - RING)
                            pool.wait_ge(idx_loaded[slot], 16 * uses(l, turn))
                            pool.sem_inc(passed, 1)
                            for t in range(K):
                                nc.gpsimd.indirect_dma_start(
                                    rows[:, slot, t, 0:D], None, table,
                                    bass.IndirectOffsetOnAxis(ap=src_idx[:, slot, t:t + 1], axis=0),
                                ).then_inc(gathered[slot], 16)

                    turns(pool, body)

            def anything():
                for l in range(L):
                    if l > 0:
                        pool.wait_ge(block_stored, 16 * BLOCKS * l)
                    pool.wait_ge(emptied, 16 * (BLOCKS + 1) * (l + 1))
                    table = node_table(l)[0:DUMP, :]

                    def body(tile, c, short):
                        pool.wait_ge(tile_loaded[l], 48 * (tile + 1))
                        pool.sem_inc(passed, 1)
                        for to, what, index in ((rows[:, 0, 0, 0:D], table, tile_src),
                                                (rows[:, 0, 0, C_HOT:C_ROW], table, tile_dst),
                                                (old_sums[:], node_sums, tile_dst)):
                            nc.gpsimd.indirect_dma_start(
                                to, None, what, bass.IndirectOffsetOnAxis(ap=index[:, 0:1], axis=0),
                            ).then_inc(tile_gathered[l], 16)
                        pool.wait_ge(tile_step, len(TILE_STEPS) * c)
                        pool.sem_inc(passed, 1)
                        nc.gpsimd.indirect_dma_start(
                            node_sums, bass.IndirectOffsetOnAxis(ap=sums_row[:, 0:1], axis=0),
                            new_sums[:], None).then_inc(tile_added, 16)

                    each_tile(pool, l, body)

            by_path(pool, grouped, anything)

        SELECTED = 2 * len(SELECTORS) + 2
        NW = 16 * 4

        @block.sync
        def _(sp):
            sp.dma_start(dst_int[:], dst).then_inc(dst_loaded, 16)
            sp.dma_start(w_sb[:], weights.rearrange("l k n -> k l n")).then_inc(weights_loaded, 16)
            sp.dma_start(wr_sb[:], rel_weights.rearrange("l k n -> k l n")).then_inc(weights_loaded, 16)
            sp.dma_start(loop_sb[:], loop_weights.rearrange("l k n -> k l n")).then_inc(weights_loaded, 16)
            sp.dma_start(att_sb[:], att).then_inc(weights_loaded, 16)
            sp.wait_ge(dve_made, DVE_MASKS)
            sp.dma_start(row_masks, masks_t[:].rearrange("g m p -> g (m p)")).then_inc(masks_stored, 16)
            sp.wait_ge(masks_stored, 16)

            def grouped():
                def store(l, g, slot, n):
                    b = slot % 2
                    at = sp.value_load(base_int[0:1, bass.ds(g, 1)] if not isinstance(g, int)
                                       else base_int[0:1, g:g + 1], min_val=0, max_val=N)
                    sp.wait_ge(result_made, n)
                    sp.sem_inc(passed, 1)
                    if not (isinstance(n, int) and n == 1):
                        sp.wait_ge(stored, 16 * (n - 1))
                    sp.sem_inc(passed, 1)
                    to = out if l == L - 1 else hidden
                    sp.dma_start(to[bass.ds(at, P), :], result[b][:]).then_inc(stored, 16)

                def load(l, g, slot, n, free, short):
                    if free:
                        sp.wait_ge(summed_up, n - RING)
                        sp.sem_inc(passed, 1)
                    sp.dma_start(src_idx[:, slot, :],
                                 src[bass.ds(g, 1)].rearrange("o p t -> (o p) t")).then_inc(idx_loaded[slot], 16)
                    if not short:
                        sp.dma_start(rows[:, slot, :, D:2 * D],
                                     edge_attr[bass.ds(g * GROUP, GROUP), :]
                                     .rearrange("(p t) d -> p t d", t=K)).then_inc(rows_loaded[slot], 16)
                    else:
                        left = E - g * GROUP
                        full = left // K
                        sp.dma_start(rows[0:full, slot, :, D:2 * D],
                                     edge_attr[g * GROUP:g * GROUP + full * K, :]
                                     .rearrange("(p t) d -> p t d", t=K)).then_inc(rows_loaded[slot], 16)
                        sp.dma_start(rows[full:full + 1, slot, 0:left - full * K, D:2 * D],
                                     edge_attr[g * GROUP + full * K:E, :]
                                     .rearrange("(p t) d -> p t d", p=1)).then_inc(rows_loaded[slot], 16)
                    sp.dma_start(mask_row[0:1, slot, :], row_masks[bass.ds(g, 1), :]).then_inc(mask_loaded[slot], 16)
                    at = sp.value_load(base_int[0:1, bass.ds(g, 1)] if not isinstance(g, int)
                                       else base_int[0:1, g:g + 1], min_val=0, max_val=N)
                    sp.dma_start(window[:, slot, :],
                                 node_table(l)[bass.ds(at, P), :]).then_inc(window_loaded[slot], 16)
                    if l == L - 1:
                        if not (isinstance(g, int) and g < RING):
                            sp.wait_ge(summed_made, n - l * G - RING)
                            sp.sem_inc(passed, 1)
                        sp.dma_start(residual[:, slot, :], x[bass.ds(at, P), :]).then_inc(residual_loaded[slot], 16)

                for l in range(L):
                    if l > 0:
                        sp.wait_ge(stored, 16 * G * l)

                    def body(turn, first, last):
                        for slot in range(RING):
                            g = RING * turn + slot
                            n = l * G + g + 1
                            if not first:
                                store(l, g - RING, slot, n - RING)
                            load(l, g, slot, n, not (first and l == 0), last and slot == RING - 1)

                    turns(sp, body)
                    for slot in range(RING):
                        store(l, G - RING + slot, slot, (l + 1) * G - RING + slot + 1)
                sp.wait_ge(stored, 16 * G * L)

            def anything():
                flat = src.rearrange("g p (t o) -> (g p t) o", o=1)
                for l in range(L):
                    if l > 0:
                        sp.wait_ge(block_stored, 16 * BLOCKS * l)
                    with sp.Fori(0, BLOCKS + 1) as blk:
                        sp.dma_start(node_sums[bass.ds(blk * P, P), :], empty_sums[:]).then_inc(emptied, 16)

                    def load(tile, c, short):
                        wide_rows = E - FULL_TILES * P if short else P
                        sp.dma_start(tile_src[:], flat[bass.ds(tile * P, P), :]).then_inc(tile_loaded[l], 16)
                        sp.dma_start(tile_dst[:], dst_flat[bass.ds(tile * P, P), :]).then_inc(tile_loaded[l], 16)
                        sp.dma_start(rows[0:wide_rows, 0, 0, D:2 * D],
                                     edge_attr[bass.ds(tile * P, wide_rows), :]).then_inc(tile_loaded[l], 16)
                        sp.wait_ge(tile_added, 16 * c)
                        sp.sem_inc(passed, 1)

                    each_tile(sp, l, load)

                    def block_pass(blk, c):
                        at = bass.ds(blk * P, P)
                        sp.dma_start(old_sums[:], node_sums[at, :]).then_inc(block_loaded, 16)
                        sp.dma_start(window[:, 0, :], node_table(l)[at, :]).then_inc(block_loaded, 16)
                        sp.dma_start(residual[:, 0, :], x[at, :]).then_inc(block_loaded, 16)
                        sp.wait_ge(block_step, len(BLOCK_STEPS) * c)
                        sp.sem_inc(passed, 1)
                        to = out if l == L - 1 else hidden
                        sp.dma_start(to[at, :], result[0][:]).then_inc(block_stored, 16)
                        sp.wait_ge(block_stored, 16 * c)
                        sp.sem_inc(passed, 1)

                    each_block(sp, l, block_pass)

            by_path(sp, grouped, anything)

        @block.vector
        def _(dve):
            made = [0]

            def step(ins):
                made[0] += 1
                ins.then_inc(dve_made, 1)
                dve.wait_ge(dve_made, made[0])

            V = nc.vector
            step(V.memset(ones[:], 1.0))
            step(V.memset(eps[:], EPS))
            step(V.memset(rows[:, :, :, C_ONE:C_ONE + 1], 1.0))
            step(V.memset(carry_m[0][:], 0.0))
            step(V.memset(carry_m[1][:], 0.0))
            step(V.memset(last_before[:], -1.0))
            step(V.memset(faults[:], 0.0))
            step(V.memset(carry_pen[:], -BIG))
            assert made[0] == DVE_ONES
            dve.wait_ge(dst_loaded, 16)
            step(V.tensor_copy(dst_f[:], dst_int[:]))
            step(V.tensor_copy(last_before[:, 1:G], dst_f[:, 0:G - 1, K - 1]))
            assert made[0] == DVE_DST
            dve.wait_ge(pe_made, 1)
            step(V.tensor_copy(base[:], ps_row[:, 0:G]))
            step(V.tensor_copy(base_int[:], base[0:1, :]))
            step(V.tensor_tensor(rel[:], dst_f[:], base[:].unsqueeze(2).broadcast_to([P, G, K]), ALU.subtract))
            step(V.tensor_tensor(base_step[:, 1:G], base[:, 1:G], base[:, 0:G - 1], ALU.subtract))
            step(V.tensor_copy(firsts_t[:], ps_out[0:G, 0:P]))
            step(V.tensor_copy(lasts_t[:], ps_out[0:G, P:2 * P]))
            step(V.tensor_copy(before_t[:], ps_out[0:G, 2 * P:3 * P]))
            assert made[0] == DVE_TURNED
            step(V.memset(masks_t[:], -BIG))
            step(V.tensor_tensor(spans_t[:], firsts_t[:], lasts_t[:], ALU.not_equal))
            step(V.tensor_scalar(spans_t[:], spans_t[:], -BIG, None, ALU.mult))
            step(V.tensor_tensor(masks_t[:, 0, 1:P], lasts_t[:, 0:P - 1], firsts_t[:, 1:P], ALU.not_equal))
            step(V.tensor_tensor(masks_t[:, 0, 0:1], before_t[:, P - 1:P], firsts_t[:, 0:1], ALU.not_equal))
            step(V.tensor_scalar(masks_t[:, 0, :], masks_t[:, 0, :], -BIG, None, ALU.mult))
            step(V.tensor_tensor(masks_t[:, 1, 1:P], masks_t[:, 0, 1:P], spans_t[:, 0:P - 1], ALU.add))
            step(V.tensor_copy(masks_t[:, 2, 0:P - 1], masks_t[:, 0, 1:P]))
            step(V.tensor_tensor(masks_t[:, 3, 0:P - 1], masks_t[:, 2, 0:P - 1], spans_t[:, 1:P], ALU.add))
            step(V.memset(step_pen[:], 0.0))
            assert made[0] == DVE_MASKS
            step(V.tensor_tensor(step_pen[:, :, 1:K], dst_f[:, :, 1:K], dst_f[:, :, 0:K - 1], ALU.not_equal))
            step(V.tensor_scalar(step_pen[:], step_pen[:], -BIG, None, ALU.mult))
            step(V.tensor_copy(back_pen[:], step_pen[:, :, K:0:-1]))
            step(V.tensor_tensor(head_pen[:], dst_f[:], dst_f[:, :, 0:1].broadcast_to([P, G, K]), ALU.not_equal))
            step(V.tensor_scalar(head_pen[:], head_pen[:], -BIG, None, ALU.mult))
            step(V.tensor_tensor(tail_pen[:], dst_f[:], dst_f[:, :, K - 1:K].broadcast_to([P, G, K]),
                                 ALU.not_equal))
            step(V.tensor_scalar(tail_pen[:], tail_pen[:], -BIG, None, ALU.mult))
            dve.wait_ge(selectors, SELECTED)
            step(V.tensor_scalar(carry_pen[:, 1:G], base_step[:, 1:G], partition[:, 0:1], -BIG,
                                 ALU.not_equal, ALU.mult))
            step(V.tensor_tensor(unsorted[:, :, 0:K - 1], dst_f[:, :, 0:K - 1], dst_f[:, :, 1:K], ALU.is_gt))
            step(V.tensor_reduce(faults[:, 0:1], unsorted[:, :, 0:K - 1], AX.XY, ALU.max))
            step(V.tensor_tensor(spans_t[:, 0:P - 1], lasts_t[:, 0:P - 1], firsts_t[:, 1:P], ALU.is_gt))
            step(V.tensor_tensor(spans_t[:, P - 1:P], before_t[:, P - 1:P], firsts_t[:, 0:1], ALU.is_gt))
            step(V.tensor_reduce(faults[0:G, 1:2], spans_t[:], AX.X, ALU.max))
            step(V.tensor_scalar(base_step[:, 0:1], base[:, G - 1:G], -1.0, float(N - 1), ALU.mult, ALU.add))
            step(V.tensor_scalar(wide[:], base_step[:], float(P - 1), None, ALU.is_gt))
            step(V.tensor_reduce(faults[:, 2:3], wide[:], AX.X, ALU.max))
            step(V.tensor_scalar(faults[:, 3:4], base[:, 0:1], 0.0, None, ALU.is_gt))
            dve.wait_ge(weights_loaded, NW)
            for l in range(L):
                for c in range(3):
                    ins = V.tensor_scalar(att_wide[:, l, c, :], ones[:], att_sb[:, 3 * l + c:3 * l + c + 1],
                                          None, ALU.mult)
            step(ins)
            assert made[0] == DVE_ATT
            dve.wait_ge(pe_made, 2)
            step(V.tensor_copy(w_turned[:], ps_turn[:, 0:L * D].rearrange("p (l d) -> p l d", l=L)))
            step(V.tensor_copy(wr_turned[:], ps_turn[:, L * D:2 * L * D].rearrange("p (l d) -> p l d", l=L)))
            dve.wait_ge(pe_made, 3)
            for l in range(L):
                V.tensor_copy(w_loop[:, l, :], ps_sum[l][:, 0:D])
                for b in range(2):
                    V.memset(score_w[l][b][:, C_ONE:C_ONE + 1], 0.0)
                    V.tensor_copy(score_w[l][b][:, 0:2 * D], ps_sum[l][:, D:3 * D])
                V.tensor_copy(score_w[l][0][:, C_HOT:C_ROW], ps_turn[:, l * D:(l + 1) * D])
                ins = V.tensor_scalar(dst_wide[:, l, :], ones[:], ps_win[l][:, 0:1], None, ALU.mult)
            step(ins)
            step(V.tensor_reduce(fault_row[:], ps_col[0:1, 0:4], AX.X, ALU.max))
            step(V.tensor_scalar(fault_row[:], fault_row[:], 1.0, None, ALU.min))
            step(V.tensor_scalar(below[:], column[:], partition[:, 0:1], None, ALU.is_lt))
            step(V.memset(empty_sums[:], 0.0))
            step(V.memset(empty_sums[:, C_HOT:C_HOT + 1], -BIG))
            V.tensor_copy(general[:], fault_row[:]).then_inc(general_ready, 1)
            assert made[0] == DVE_ALL, made[0]

            def grouped():
                def hots(slot, turn, tiles):
                    for t in tiles:
                        g = RING * turn + slot
                        at = rel[:, bass.ds(g, 1), t:t + 1].rearrange("p o t -> p (o t)")
                        ins = V.tensor_scalar(rows[:, slot, t, C_HOT:C_ROW], column[:], at, None, ALU.is_equal)
                    ins.then_inc(hot_made, 1)

                for l in range(L):
                    def body(turn, first, last):
                        for slot in range(RING):
                            g = RING * turn + slot
                            n = l * G + g + 1
                            b = slot % 2
                            start = first and slot == 0
                            end = last and slot == RING - 1
                            next_slot, next_turn = (slot + 1) % RING, turn + (slot + 1) // RING
                            if start:
                                if l > 0:
                                    dve.wait_ge(summed_up, n - 1)
                                hots(0, 0, range(HALF_A))
                                hots(0, 0, range(HALF_A, K))
                            dve.wait_ge(hot_made, 2 * n)
                            dve.wait_ge(rows_loaded[slot], 16 * row_uses(l, turn, slot, end))
                            dve.wait_ge(gathered[slot], 16 * K * uses(l, turn))
                            dve.wait_ge(score_w_made, n)
                            for t in range(K):
                                ins = V.tensor_tensor_reduce(products[:, t, :], rows[:, slot, t, 0:C_ROW],
                                                             score_w[l][b][:], 1.0, 0.0, ALU.mult, ALU.add,
                                                             score_raw[:, b, t:t + 1])
                            ins.then_inc(raw_made, 1)
                            dve.wait_ge(raw_made, n)
                            V.scalar_tensor_tensor(score[:, b, :], score_raw[:, b, :], NEG_SLOPE,
                                                   score_raw[:, b, :], ALU.mult, ALU.max).then_inc(score_made, 1)
                            dve.wait_ge(score_made, n)
                            fwd_pen = step_pen[:, bass.ds(g, 1), 0:K].rearrange("p o t -> p (o t)")
                            bwd_pen = back_pen[:, bass.ds(g, 1), :].rearrange("p o t -> p (o t)")
                            V.tensor_tensor_scan(run_fwd[:, b, :], fwd_pen, score[:, b, :], -BIG,
                                                 ALU.add, ALU.max)
                            V.tensor_tensor_scan(run_bwd[:, b, ::-1], bwd_pen, score[:, b, ::-1], -BIG,
                                                 ALU.add, ALU.max).then_inc(runs_made, 1)
                            if not start:
                                reciprocal_total(l, n - 1, 1 - b)
                            if not end:
                                if not (l == 0 and first and slot < RING - 1):
                                    dve.wait_ge(summed_up, n + 1 - RING)
                                hots(next_slot, next_turn, range(HALF_A))
                            if l == L - 1 and not start:
                                normalise_a(slot - 1 if slot else RING - 1, n - 1, turn if slot else turn - 1, l)
                            dve.wait_ge(row_ready, n)
                            V.tensor_tensor_scan(carried[0:1, b, 0:P], mask_row[0:1, slot, P:2 * P],
                                                 ps_row[0:1, 0:P], -BIG, ALU.add, ALU.max)
                            V.tensor_tensor_scan(carried[0:1, b, 2 * P - 1:P - 1:-1],
                                                 mask_row[0:1, slot, 4 * P - 1:3 * P - 1:-1],
                                                 ps_row[0:1, 2 * P - 1:P - 1:-1], -BIG,
                                                 ALU.add, ALU.max).then_inc(carried_made, 1)
                            if not end:
                                hots(next_slot, next_turn, range(HALF_A, K))
                            dve.wait_ge(runs_made, n)
                            V.tensor_tensor(peak_a[:, b, :], run_fwd[:, b, :], run_bwd[:, b, :],
                                            ALU.max).then_inc(peak_a_made, 1)
                            dve.wait_ge(peak_a_made, n)
                            dve.wait_ge(col_ready, n)
                            hp = head_pen[:, bass.ds(g, 1), :].rearrange("p o t -> p (o t)")
                            tp = tail_pen[:, bass.ds(g, 1), :].rearrange("p o t -> p (o t)")
                            V.scalar_tensor_tensor(peak_b[:, b, :], hp, ps_col[:, 0:1], peak_a[:, b, :],
                                                   ALU.add, ALU.max).then_inc(peak_b_made, 1)
                            dve.wait_ge(peak_b_made, n)
                            V.scalar_tensor_tensor(peak[:, b, :], tp, ps_col[:, 1:2], peak_b[:, b, :],
                                                   ALU.add, ALU.max).then_inc(peak_made, 1)
                            dve.wait_ge(peak_made, n)
                            V.tensor_tensor(lowered[:, b, :], score[:, b, :], peak[:, b, :],
                                            ALU.subtract).then_inc(lowered_made, 1)
                            if l == L - 1 and not start:
                                normalise_b(slot - 1 if slot else RING - 1, n - 1, l)
                            dve.wait_ge(drop_ready, n)
                            V.tensor_scalar(drop[:, b:b + 1], ps_col[:, 2:3], 0.0, None,
                                            ALU.min).then_inc(drop_made, 1)

                    def reciprocal_total(l, n, b):
                        dve.wait_ge(summed_up, n)
                        V.tensor_scalar(total[:, b:b + 1], ps_sum[b][:, C_ONE:C_ONE + 1], TINY, None,
                                        ALU.max).then_inc(total_made, 1)
                        dve.wait_ge(total_made, n)
                        V.reciprocal(inv_total[:, b:b + 1], total[:, b:b + 1]).then_inc(inv_total_made, 1)

                    def normalise_a(slot, n, turn, l):
                        b = slot % 2
                        m = n - l * G
                        dve.wait_ge(out_ready, n)
                        dve.wait_ge(residual_loaded[slot], 16 * (turn + 1))
                        V.scalar_tensor_tensor(summed[b][:], ps_out[:, 0:D], 0.0, residual[:, slot, :],
                                               ALU.max, ALU.add).then_inc(summed_made, 1)
                        dve.wait_ge(summed_made, m)
                        V.bn_stats(stats[:, b, :], summed[b][:]).then_inc(stats_made, 1)
                        dve.wait_ge(stats_made, m)
                        dve.sem_inc(passed, 1)
                        V.bn_aggr(mean_var[:, b, :], stats[:, b, :]).then_inc(mean_var_made, 1)

                    def normalise_b(slot, n, l):
                        b = slot % 2
                        m = n - l * G
                        dve.wait_ge(inv_std_made, m)
                        if not (isinstance(m, int) and m <= 2):
                            dve.wait_ge(stored, 16 * (n - 2))
                        V.tensor_scalar(result[b][:], summed[b][:], mean_var[:, b, 0:1], inv_std[:, b:b + 1],
                                        ALU.subtract, ALU.mult).then_inc(result_made, 1)

                    turns(dve, body)
                    n_last = (l + 1) * G
                    reciprocal_total(l, n_last, (G - 1) % 2)
                    if l == L - 1:
                        normalise_a((G - 1) % RING, n_last, TURNS - 1, l)
                        normalise_b((G - 1) % RING, n_last, l)

            def anything():
                col = {n: tile_work[:, i:i + 1] for i, n in enumerate(
                    ("raw", "score", "tile_peak", "new_peak", "lowered", "old_lowered", "repeats",
                     "alpha", "old_scale", "is_repeat", "dump_gap", "row_float"))}

                for l in range(L):
                    def tile_pass(tile, c, short):
                        dve.wait_ge(tile_loaded[l], 48 * (tile + 1))
                        V.tensor_copy(tile_dst_f[:], tile_dst[:]).then_inc(tile_step, 1)
                        dve.wait_ge(tile_gathered[l], 48 * (tile + 1))
                        dve.wait_ge(tile_step, tile_before("raw", c))
                        V.tensor_tensor_reduce(products[:, 0, :], rows[:, 0, 0, 0:C_ROW], score_w[l][0][:],
                                               1.0, 0.0, ALU.mult, ALU.add, col["raw"]).then_inc(tile_step, 1)
                        dve.wait_ge(tile_step, tile_before("score", c))
                        V.scalar_tensor_tensor(col["score"], col["raw"], NEG_SLOPE, col["raw"],
                                               ALU.mult, ALU.max).then_inc(tile_step, 1)
                        dve.wait_ge(tile_step, tile_before("spread_score", c))
                        V.tensor_scalar(spread[:, 0, :], ones[:], col["score"], None,
                                        ALU.mult).then_inc(tile_step, 1)
                        dve.wait_ge(tile_step, tile_before("spread_dst", c))
                        V.tensor_scalar(spread[:, 1, :], ones[:], tile_dst_f[:], None,
                                        ALU.mult).then_inc(tile_step, 1)
                        dve.wait_ge(tile_step, tile_before("other_pen", c))
                        V.tensor_scalar(other_pen[:], ps_row[:, P:2 * P], tile_dst_f[:], -BIG,
                                        ALU.not_equal, ALU.mult).then_inc(tile_step, 1)
                        dve.wait_ge(tile_step, tile_before("same", c))
                        V.tensor_scalar(same[:], ps_row[:, P:2 * P], tile_dst_f[:], None,
                                        ALU.is_equal).then_inc(tile_step, 1)
                        dve.wait_ge(tile_step, tile_before("masked", c))
                        V.tensor_tensor(masked[:], other_pen[:], ps_row[:, 0:P], ALU.add).then_inc(tile_step, 1)
                        dve.wait_ge(tile_step, tile_before("tile_peak", c))
                        V.tensor_reduce(col["tile_peak"], masked[:], AX.X, ALU.max).then_inc(tile_step, 1)
                        dve.wait_ge(tile_step, tile_before("new_peak", c))
                        V.tensor_tensor(col["new_peak"], col["tile_peak"], old_sums[:, C_HOT:C_HOT + 1],
                                        ALU.max).then_inc(tile_step, 1)
                        dve.wait_ge(tile_step, tile_before("lowered", c))
                        V.tensor_tensor(col["lowered"], col["score"], col["new_peak"],
                                        ALU.subtract).then_inc(tile_step, 1)
                        dve.wait_ge(tile_step, tile_before("old_lowered", c))
                        V.tensor_tensor(col["old_lowered"], old_sums[:, C_HOT:C_HOT + 1], col["new_peak"],
                                        ALU.subtract).then_inc(tile_step, 1)
                        dve.wait_ge(tile_step, tile_before("repeats", c))
                        V.tensor_tensor_reduce(products[:, 1, 0:P], same[:], below[:], 1.0, 0.0,
                                               ALU.mult, ALU.add, col["repeats"]).then_inc(tile_step, 1)
                        dve.wait_ge(tile_step, tile_before("new_sums", c))
                        V.scalar_tensor_tensor(new_sums[:, 0:C_HOT], old_sums[:, 0:C_HOT], col["old_scale"],
                                               ps_sum[0][:, 0:C_HOT], ALU.mult, ALU.add).then_inc(tile_step, 1)
                        dve.wait_ge(tile_step, tile_before("keep_peak", c))
                        V.tensor_copy(new_sums[:, C_HOT:C_HOT + 1], col["new_peak"]).then_inc(tile_step, 1)
                        dve.wait_ge(tile_step, tile_before("is_repeat", c))
                        V.tensor_scalar(col["is_repeat"], col["repeats"], 0.5, None,
                                        ALU.is_gt).then_inc(tile_step, 1)
                        dve.wait_ge(tile_step, tile_before("dump_gap", c))
                        V.scalar_tensor_tensor(col["dump_gap"], partition[:], float(DUMP), tile_dst_f[:],
                                               ALU.add, ALU.subtract).then_inc(tile_step, 1)
                        dve.wait_ge(tile_step, tile_before("row_float", c))
                        V.scalar_tensor_tensor(col["row_float"], col["dump_gap"], col["is_repeat"],
                                               tile_dst_f[:], ALU.mult, ALU.add).then_inc(tile_step, 1)
                        dve.wait_ge(tile_step, tile_before("row_int", c))
                        V.tensor_copy(sums_row[:], col["row_float"]).then_inc(tile_step, 1)

                    each_tile(dve, l, tile_pass)

                    def block_pass(blk, c):
                        dve.wait_ge(block_loaded, 48 * c)
                        V.tensor_scalar(total[:, 0:1], old_sums[:, C_ONE:C_ONE + 1], TINY, None,
                                        ALU.max).then_inc(block_step, 1)
                        dve.wait_ge(block_step, block_before("inverse", c))
                        V.reciprocal(inv_total[:, 0:1], total[:, 0:1]).then_inc(block_step, 1)
                        if l < L - 1:
                            dve.wait_ge(block_step, block_before("relu", c))
                            V.tensor_scalar(result[0][:], ps_out[:, 0:D], 0.0, None, ALU.max).then_inc(
                                block_step, BLOCK_STEPS.index("normalise") - BLOCK_STEPS.index("relu") + 1)
                            return
                        dve.wait_ge(block_step, block_before("relu", c))
                        V.scalar_tensor_tensor(summed[0][:], ps_out[:, 0:D], 0.0, residual[:, 0, :],
                                               ALU.max, ALU.add).then_inc(block_step, 1)
                        dve.wait_ge(block_step, block_before("stats", c))
                        V.bn_stats(stats[:, 0, :], summed[0][:]).then_inc(block_step, 1)
                        dve.wait_ge(block_step, block_before("aggregate", c))
                        dve.sem_inc(passed, 1)
                        V.bn_aggr(mean_var[:, 0, :], stats[:, 0, :]).then_inc(block_step, 1)
                        dve.wait_ge(block_step, block_before("normalise", c))
                        V.tensor_scalar(result[0][:], summed[0][:], mean_var[:, 0, 0:1], inv_std[:, 0:1],
                                        ALU.subtract, ALU.mult).then_inc(block_step, 1)

                    each_block(dve, l, block_pass)

            by_path(dve, grouped, anything)

        @block.tensor
        def _(pe):
            T = nc.tensor
            pe.wait_ge(selectors, SELECTED)
            pe.wait_ge(dve_made, DVE_DST)
            T.matmul(ps_row[:, 0:G], from_first[:], dst_f[:, :, 0], start=True, stop=True)
            T.transpose(ps_out[0:G, 0:P], dst_f[:, :, 0], identity[:])
            T.transpose(ps_out[0:G, P:2 * P], dst_f[:, :, K - 1], identity[:])
            T.transpose(ps_out[0:G, 2 * P:3 * P], last_before[:], identity[:]).then_inc(pe_made, 1)
            pe.wait_ge(weights_loaded, NW)
            for l in range(L):
                T.transpose(ps_turn[:, l * D:(l + 1) * D], w_sb[:, l, :], identity[:])
            for l in range(L):
                ins = T.transpose(ps_turn[:, (L + l) * D:(L + l + 1) * D], wr_sb[:, l, :], identity[:])
            ins.then_inc(pe_made, 1)
            pe.wait_ge(dve_made, DVE_ATT + 2)
            for l in range(L):
                T.matmul(ps_sum[l][:, 0:D], w_turned[:, l, :], loop_sb[:, l, :], start=True, stop=True)
                T.matmul(ps_sum[l][:, D:2 * D], att_wide[:, l, 0, :], w_turned[:, l, :], start=True, stop=True)
                T.matmul(ps_sum[l][:, 2 * D:3 * D], att_wide[:, l, 2, :], wr_turned[:, l, :], start=True, stop=True)
                T.matmul(ps_turn[:, l * D:(l + 1) * D], att_wide[:, l, 1, :], w_turned[:, l, :],
                         start=True, stop=True)
                T.matmul(ps_win[l][:, 0:1], w_turned[:, l, :], att_sb[:, 3 * l + 1:3 * l + 2], start=True, stop=True)
            T.matmul(ps_col[0:1, 0:4], ones[:, 0:1], faults[:], start=True, stop=True).then_inc(pe_made, 1)
            pe.wait_ge(dve_made, DVE_ALL)

            def grouped():
                def prepare(l, slot, n, turn):
                    b = slot % 2
                    pe.wait_ge(window_loaded[slot], 16 * uses(l, turn))
                    T.transpose(ps_win[b][:, 0:D], window[:, slot, :], identity[:]).then_inc(window_turned, 1)
                    pe.wait_ge(window_t_made, n)
                    T.matmul(ps_win[b][:, D:D + P], dst_wide[:, l, :], window_t[:, slot, :],
                             start=True, stop=True).then_inc(dst_scored, 1)

                def finish(l, slot, n):
                    pe.wait_ge(mean_made, n)
                    for h in range(2):
                        ins = T.transpose(ps_turn[:, h * D:(h + 1) * D], mean_rows[:, h * D:(h + 1) * D], identity[:])
                    ins.then_inc(mean_turned, 1)
                    pe.wait_ge(mean_t_made, n)
                    T.matmul(ps_out[:, 0:D], window_t[:, slot, :], w_loop[:, l, :], start=True, stop=False)
                    T.matmul(ps_out[:, 0:D], mean_t[:, 0:D], w_sb[:, l, :], start=False, stop=False)
                    T.matmul(ps_out[:, 0:D], mean_t[:, D:2 * D], wr_sb[:, l, :],
                             start=False, stop=True).then_inc(out_ready, 1)

                for l in range(L):
                    def body(turn, first, last):
                        for slot in range(RING):
                            n = l * G + RING * turn + slot + 1
                            b = slot % 2
                            start = first and slot == 0
                            end = last and slot == RING - 1
                            if start:
                                prepare(l, 0, n, turn)
                            if not end:
                                prepare(l, (slot + 1) % RING, n + 1, turn + (slot + 1) // RING)
                            if not start:
                                finish(l, (slot - 1) % RING, n - 1)
                            pe.wait_ge(runs_made, n)
                            pe.wait_ge(mask_loaded[slot], 16 * uses(l, turn))
                            T.matmul(ps_row[0:1, 0:P], run_fwd[:, b, K - 1:K], shift_down[:], start=True, stop=False)
                            if not start:
                                T.matmul(ps_row[0:1, 0:P], peak[:, 1 - b, K - 1:K], last_to_first[:],
                                         start=False, stop=False)
                            T.matmul(ps_row[0:1, 0:P], ones[0:1, 0:1], mask_row[0:1, slot, 0:P],
                                     start=False, stop=True)
                            T.matmul(ps_row[0:1, P:2 * P], run_bwd[:, b, 0:1], shift_up[:], start=True, stop=False)
                            T.matmul(ps_row[0:1, P:2 * P], ones[0:1, 0:1], mask_row[0:1, slot, 2 * P:3 * P],
                                     start=False, stop=True).then_inc(row_ready, 1)
                            pe.wait_ge(carried_made, n)
                            for c in range(2):
                                ins = T.matmul(ps_col[:, c:c + 1], carried[0:1, b, c * P:(c + 1) * P],
                                               ones[0:1, 0:1], start=True, stop=True)
                            ins.then_inc(col_ready, 1)
                            pe.wait_ge(peak_made, n)
                            if not start:
                                T.matmul(ps_col[:, 2:3], from_last[:], peak[:, 1 - b, K - 1:K], start=True, stop=False)
                                T.matmul(ps_col[:, 2:3], minus_first[:], peak[:, b, 0:1],
                                         start=False, stop=True).then_inc(drop_ready, 1)
                            else:
                                T.matmul(ps_col[:, 2:3], minus_first[:], peak[:, b, 0:1],
                                         start=True, stop=True).then_inc(drop_ready, 1)
                            if not start:
                                pe.wait_ge(carry_made, n)
                                pe.wait_ge(sums_made, n - 1)
                                T.matmul(ps_sum[b][:, 0:C_HOT], carry_m[b][:], sums[1 - b][:], start=True, stop=False)
                            for t in range(K):
                                pe.wait_ge(weighted_made, K * (n - 1) + t + 1)
                                ins = T.matmul(ps_sum[b][:, 0:C_HOT], weighted[:, b, t, :],
                                               rows[:, slot, t, 0:C_HOT], start=start and t == 0, stop=t == K - 1)
                            ins.then_inc(summed_up, 1)

                    turns(pe, body)
                    finish(l, (G - 1) % RING, (l + 1) * G)

            def anything():
                for l in range(L):
                    def tile_pass(tile, c, short):
                        pe.wait_ge(tile_step, tile_before("lay_out", c))
                        T.matmul(ps_row[:, 0:P], spread[:, 0, :], identity[:], start=True, stop=True)
                        T.matmul(ps_row[:, P:2 * P], spread[:, 1, :], identity[:],
                                 start=True, stop=True).then_inc(tile_step, 1)
                        pe.wait_ge(tile_step, tile_before("add_up", c))
                        T.matmul(ps_sum[0][:, 0:C_HOT], same[:], tile_rows[:],
                                 start=True, stop=True).then_inc(tile_step, 1)

                    each_tile(pe, l, tile_pass)

                    def block_pass(blk, c):
                        pe.wait_ge(block_step, block_before("turn", c))
                        for h in range(2):
                            T.transpose(ps_turn[:, h * D:(h + 1) * D], mean_rows[:, h * D:(h + 1) * D],
                                        identity[:])
                        T.transpose(ps_win[0][:, 0:D], window[:, 0, :], identity[:]).then_inc(block_step, 1)
                        pe.wait_ge(block_step, block_before("product", c))
                        T.matmul(ps_out[:, 0:D], window_t[:, 0, :], w_loop[:, l, :], start=True, stop=False)
                        T.matmul(ps_out[:, 0:D], mean_t[:, 0:D], w_sb[:, l, :], start=False, stop=False)
                        T.matmul(ps_out[:, 0:D], mean_t[:, D:2 * D], wr_sb[:, l, :],
                                 start=False, stop=True).then_inc(block_step, 1)

                    each_block(pe, l, block_pass)

            by_path(pe, grouped, anything)

        @block.scalar
        def _(act):
            A = nc.scalar
            act.wait_ge(dve_made, DVE_ALL)

            def grouped():
                def window_copy(l, slot, n):
                    act.wait_ge(window_turned, n)
                    A.activation(window_t[:, slot, :], ps_win[slot % 2][:, 0:D], ACT.Copy).then_inc(window_t_made, 1)

                def score_copy(l, slot, n):
                    act.wait_ge(dst_scored, n)
                    A.activation(score_w[l][slot % 2][:, C_HOT:C_ROW], ps_win[slot % 2][:, D:D + P],
                                 ACT.Copy).then_inc(score_w_made, 1)

                def averages(n, b):
                    act.wait_ge(inv_total_made, n)
                    A.activation(mean_rows[:], ps_sum[b][:, 0:2 * D], ACT.Copy,
                                 scale=inv_total[:, b:b + 1]).then_inc(mean_made, 1)
                    A.activation(sums[b][:], ps_sum[b][:, 0:C_HOT], ACT.Copy).then_inc(sums_made, 1)

                def averages_turned(n):
                    act.wait_ge(mean_turned, n)
                    A.activation(mean_t[:], ps_turn[:, 0:2 * D], ACT.Copy).then_inc(mean_t_made, 1)

                def output(l, n, b):
                    if l < L - 1:
                        act.wait_ge(out_ready, n)
                        if not (isinstance(n, int) and n <= 2):
                            act.wait_ge(stored, 16 * (n - 2))
                        A.activation(result[b][:], ps_out[:, 0:D], ACT.Relu).then_inc(result_made, 1)
                    else:
                        m = n - l * G
                        act.wait_ge(mean_var_made, m)
                        A.activation(log_var[:, b:b + 1], mean_var[:, b, 1:2], ACT.Ln,
                                     bias=eps[:]).then_inc(log_var_made, 1)
                        act.wait_ge(log_var_made, m)
                        A.activation(inv_std[:, b:b + 1], log_var[:, b:b + 1], ACT.Exp,
                                     scale=-0.5).then_inc(inv_std_made, 1)

                for l in range(L):
                    def body(turn, first, last):
                        for slot in range(RING):
                            g = RING * turn + slot
                            n = l * G + g + 1
                            b = slot % 2
                            start = first and slot == 0
                            end = last and slot == RING - 1
                            if start:
                                window_copy(l, 0, n)
                                score_copy(l, 0, n)
                            if not end:
                                window_copy(l, (slot + 1) % RING, n + 1)
                                score_copy(l, (slot + 1) % RING, n + 1)
                            if not start:
                                averages(n - 1, 1 - b)
                                averages_turned(n - 1)
                                output(l, n - 1, 1 - b)
                            act.wait_ge(lowered_made, n)
                            A.activation(alpha[:, b, :], lowered[:, b, :], ACT.Exp).then_inc(alpha_made, 1)
                            act.wait_ge(drop_made, n)
                            pen = carry_pen[:, bass.ds(g, 1)]
                            A.activation(carry_m[b][:, 0:1], drop[:, b:b + 1], ACT.Exp,
                                         bias=pen).then_inc(carry_made, 1)
                            act.wait_ge(alpha_made, n)
                            for t in range(K):
                                A.activation(weighted[:, b, t, :], rows[:, slot, t, C_HOT:C_ROW], ACT.Copy,
                                             scale=alpha[:, b, t:t + 1]).then_inc(weighted_made, 1)

                    turns(act, body)
                    averages((l + 1) * G, (G - 1) % 2)
                    averages_turned((l + 1) * G)
                    output(l, (l + 1) * G, (G - 1) % 2)

            def anything():
                alpha_col, old_scale = tile_work[:, 7:8], tile_work[:, 8:9]
                for l in range(L):
                    def tile_pass(tile, c, short):
                        act.wait_ge(tile_step, tile_before("alpha", c))
                        A.activation(alpha_col, tile_work[:, 4:5], ACT.Exp).then_inc(tile_step, 1)
                        act.wait_ge(tile_step, tile_before("old_scale", c))
                        A.activation(old_scale, tile_work[:, 5:6], ACT.Exp).then_inc(tile_step, 1)
                        act.wait_ge(tile_step, tile_before("weigh", c))
                        A.activation(tile_rows[:], rows[:, 0, 0, 0:C_HOT], ACT.Copy,
                                     scale=alpha_col).then_inc(tile_step, 1)

                    each_tile(act, l, tile_pass)

                    def block_pass(blk, c):
                        act.wait_ge(block_step, block_before("mean", c))
                        A.activation(mean_rows[:], old_sums[:, 0:2 * D], ACT.Copy,
                                     scale=inv_total[:, 0:1]).then_inc(block_step, 1)
                        act.wait_ge(block_step, block_before("mean_turned", c))
                        A.activation(mean_t[:], ps_turn[:, 0:2 * D], ACT.Copy).then_inc(block_step, 1)
                        act.wait_ge(block_step, block_before("window_turned", c))
                        A.activation(window_t[:, 0, :], ps_win[0][:, 0:D], ACT.Copy).then_inc(block_step, 1)
                        if l == L - 1:
                            act.wait_ge(block_step, block_before("log", c))
                            A.activation(log_var[:, 0:1], mean_var[:, 0, 1:2], ACT.Ln,
                                         bias=eps[:]).then_inc(block_step, 1)
                            act.wait_ge(block_step, block_before("inv_std", c))
                            A.activation(inv_std[:, 0:1], log_var[:, 0:1], ACT.Exp,
                                         scale=-0.5).then_inc(block_step, 1)

                    each_block(act, l, block_pass)

            by_path(act, grouped, anything)


_IN = ("x", "src", "dst", "edge_attr_128", "L0_gnn_W", "L0_gnn_Wr", "L0_gnn_Att", "L0_gnn_Loop")


def kernel(**inputs):
    import numpy as np
    import concourse.bacc as bacc
    from concourse.bass_utils import run_bass_kernel_spmd

    x, src, dst, edge_attr, w, wr, att, loop = (np.asarray(inputs[n]) for n in _IN)
    nodes, edges, layers = x.shape[0], src.shape[0], w.shape[0]
    tiles = -(-edges // P)
    groups = -(-tiles // (K * RING)) * RING
    padded = groups * K * P
    src_pad = np.pad(src, (0, padded - edges)).reshape(groups, P, K)
    dst_pad = np.pad(dst, (0, padded - edges), constant_values=nodes).reshape(groups, P, K)
    arrays = {
        "x": np.pad(x, ((0, P), (0, 0))),
        "src": src_pad,
        "dst": np.ascontiguousarray(dst_pad.transpose(1, 0, 2)),
        "dst_flat": dst_pad.reshape(padded, 1),
        "edge_attr": edge_attr,
        "weights": w,
        "rel_weights": wr,
        "att": np.ascontiguousarray(att.reshape(layers, 3, D).transpose(2, 0, 1).reshape(D, layers * 3)),
        "loop_weights": loop,
    }
    nc = bacc.Bacc("TRN2", target_bir_lowering=False, num_devices=1)
    args = [nc.dram_tensor(n, a.shape, mybir.dt.from_np(a.dtype), kind="ExternalInput").ap()
            for n, a in arrays.items()]
    out = nc.dram_tensor("out", (nodes + P, D), F32, kind="ExternalOutput").ap()
    gnn_program(nc, *args, out, {"nodes": nodes, "edges": edges, "groups": groups, "layers": layers})
    r = run_bass_kernel_spmd(nc, [arrays], core_ids=[0])
    return r.results[0]["out"][:nodes]
```

```python
from contextlib import ExitStack

import concourse.bass as bass
from concourse import mybir


F32 = mybir.dt.float32
I32 = mybir.dt.int32
ALU = mybir.AluOpType
ACT = mybir.ActivationFunctionType
AX = mybir.AxisListType

P = 128
D = 128
K = 13
RING = 4
PARTS = ((0, 7), (7, 11), (11, K))
NEG_SLOPE = 0.01
EPS = 1e-5
BIG = 1e30
TINY = 1e-30

C_ONE = 2 * D
C_HOT = C_ONE + 1
C_ROW = C_HOT + P
C_PITCH = C_ROW + 3


def gnn_program(nc, x, src, dst, dst_flat, edge_attr, weights, rel_weights, att, loop_weights, out, plan):
    N, E, G, L = plan["nodes"], plan["edges"], plan["groups"], plan["layers"]
    GROUP = K * P
    TURNS = G // RING
    FULL_TILES = E // P
    TILES = -(-E // P)
    BLOCKS = N // P + 1
    DUMP = BLOCKS * P

    hidden = nc.dram_tensor("hidden", (N + P, D), F32, kind="Internal").ap()
    row_masks = nc.dram_tensor("row_masks", (G, 4 * P), F32, kind="Internal").ap()
    node_sums = nc.dram_tensor("node_sums", (DUMP + P, C_HOT + 1), F32, kind="Internal").ap()

    with ExitStack() as ctx:
        def sb(name, shape, dt=F32):
            return ctx.enter_context(nc.sbuf_tensor(name, shape, dt))

        def psum(name):
            return ctx.enter_context(nc.psum_tensor(name, [P, 512], F32))

        def sem(name):
            return ctx.enter_context(nc.semaphore(name))

        ones = sb("ones", [P, P])
        column = sb("column", [P, P])
        partition = sb("partition", [P, 1])
        identity = sb("identity", [P, P])
        shift_down = sb("shift_down", [P, P])
        shift_up = sb("shift_up", [P, P])
        last_to_first = sb("last_to_first", [P, P])
        from_first = sb("from_first", [P, P])
        from_last = sb("from_last", [P, P])
        minus_first = sb("minus_first", [P, P])
        eps = sb("eps", [P, 1])

        w_sb = sb("w_sb", [P, L, D])
        wr_sb = sb("wr_sb", [P, L, D])
        loop_sb = sb("loop_sb", [P, L, D])
        att_sb = sb("att_sb", [P, L * 3])
        w_turned = sb("w_turned", [P, L, D])
        wr_turned = sb("wr_turned", [P, L, D])
        w_loop = sb("w_loop", [P, L, D])
        att_wide = sb("att_wide", [P, L, 3, P])
        dst_wide = sb("dst_wide", [P, L, P])

        dst_int = sb("dst_int", [P, G, K], I32)
        dst_f = sb("dst_f", [P, G, K])
        rel = sb("rel", [P, G, K])
        last_before = sb("last_before", [P, G])
        base = sb("base", [P, G])
        base_step = sb("base_step", [P, G])
        base_int = sb("base_int", [1, G], I32)
        carry_pen = sb("carry_pen", [P, G])
        step_pen = sb("step_pen", [P, G, K + 1])
        back_pen = sb("back_pen", [P, G, K])
        head_pen = sb("head_pen", [P, G, K])
        tail_pen = sb("tail_pen", [P, G, K])
        firsts_t = sb("firsts_t", [G, P])
        lasts_t = sb("lasts_t", [G, P])
        before_t = sb("before_t", [G, P])
        masks_t = sb("masks_t", [G, 4, P])
        spans_t = sb("spans_t", [G, P])
        unsorted = sb("unsorted", [P, G, K])
        wide = sb("wide", [P, G])
        faults = sb("faults", [P, 4])
        fault_row = sb("fault_row", [1, 1])
        general = sb("general", [1, 1], I32)

        rows = sb("rows", [P, RING, K, C_PITCH])
        products = sb("products", [P, K, C_ROW])
        src_idx = sb("src_idx", [P, RING, K], I32)
        mask_row = sb("mask_row", [1, RING, 4 * P])
        window = sb("window", [P, RING, D])
        residual = sb("residual", [P, RING, D])
        window_t = sb("window_t", [P, RING, D])
        score_raw = sb("score_raw", [P, 2, K])
        score = sb("score", [P, 2, K])
        run_fwd = sb("run_fwd", [P, 2, K])
        run_bwd = sb("run_bwd", [P, 2, K])
        carried = sb("carried", [1, 2, 2 * P])
        peak_a = sb("peak_a", [P, 2, K])
        peak_b = sb("peak_b", [P, 2, K])
        peak = sb("peak", [P, 2, K])
        lowered = sb("lowered", [P, 2, K])
        alpha = sb("alpha", [P, 2, K])
        drop = sb("drop", [P, 2])
        carry_m = [sb(f"carry_m{b}", [P, P]) for b in range(2)]
        weighted = sb("weighted", [P, 2, K, P])
        sums = [sb(f"sums{b}", [P, C_HOT]) for b in range(2)]
        total = sb("total", [P, 2])
        inv_total = sb("inv_total", [P, 2])
        mean_rows = sb("mean_rows", [P, 2 * D])
        mean_t = sb("mean_t", [P, 2 * D])
        result = [sb(f"result{b}", [P, D]) for b in range(2)]
        summed = [sb(f"summed{b}", [P, D]) for b in range(2)]
        stats = sb("stats", [P, 2, 6])
        mean_var = sb("mean_var", [P, 2, 2])
        log_var = sb("log_var", [P, 2])
        inv_std = sb("inv_std", [P, 2])

        tile_src = sb("tile_src", [P, 1], I32)
        tile_dst = sb("tile_dst", [P, 1], I32)
        tile_dst_f = sb("tile_dst_f", [P, 1])
        below = sb("below", [P, P])
        spread = sb("spread", [P, 2, P])
        other_pen = sb("other_pen", [P, P])
        same = sb("same", [P, P])
        masked = sb("masked", [P, P])
        tile_work = sb("tile_work", [P, 16])
        tile_rows = sb("tile_rows", [P, C_HOT])
        old_sums = sb("old_sums", [P, C_HOT + 1])
        new_sums = sb("new_sums", [P, C_HOT + 1])
        empty_sums = sb("empty_sums", [P, C_HOT + 1])
        sums_row = sb("sums_row", [P, 1], I32)

        ps_sum = [psum(f"ps_sum{b}") for b in range(2)]
        ps_score = [psum(f"ps_score{b}") for b in range(2)]
        ps_turn = psum("ps_turn")
        ps_out = psum("ps_out")
        ps_row = psum("ps_row")
        ps_col = psum("ps_col")

        dst_loaded = sem("dst_loaded")
        weights_loaded = sem("weights_loaded")
        pool_made = sem("pool_made")
        selectors = sem("selectors")
        dve_made = sem("dve_made")
        pe_made = sem("pe_made")
        masks_stored = sem("masks_stored")
        rows_loaded = [sem(f"rows_loaded{s}") for s in range(RING)]
        idx_loaded = [sem(f"idx_loaded{s}") for s in range(RING)]
        mask_loaded = [sem(f"mask_loaded{s}") for s in range(RING)]
        window_loaded = [sem(f"window_loaded{s}") for s in range(RING)]
        residual_loaded = [sem(f"residual_loaded{s}") for s in range(RING)]
        gathered = [[sem(f"gathered{s}_{part}") for part in range(len(PARTS))] for s in range(RING)]
        hot_made = sem("hot_made")
        window_turned = sem("window_turned")
        window_t_made = sem("window_t_made")
        dst_scored = sem("dst_scored")
        raw_made = sem("raw_made")
        score_made = sem("score_made")
        runs_made = sem("runs_made")
        row_ready = sem("row_ready")
        carried_made = sem("carried_made")
        col_ready = sem("col_ready")
        peak_a_made = sem("peak_a_made")
        peak_b_made = sem("peak_b_made")
        peak_made = sem("peak_made")
        lowered_made = sem("lowered_made")
        drop_ready = sem("drop_ready")
        drop_made = sem("drop_made")
        alpha_made = sem("alpha_made")
        carry_made = sem("carry_made")
        weighted_made = sem("weighted_made")
        summed_up = sem("summed_up")
        total_made = sem("total_made")
        inv_total_made = sem("inv_total_made")
        sums_made = sem("sums_made")
        mean_made = sem("mean_made")
        mean_turned = sem("mean_turned")
        mean_t_made = sem("mean_t_made")
        out_ready = sem("out_ready")
        result_made = sem("result_made")
        summed_made = sem("summed_made")
        stats_made = sem("stats_made")
        mean_var_made = sem("mean_var_made")
        log_var_made = sem("log_var_made")
        inv_std_made = sem("inv_std_made")
        stored = sem("stored")
        general_ready = sem("general_ready")
        emptied = sem("emptied")
        score_ready = sem("score_ready")
        tile_loaded = [sem(f"tile_loaded{l}") for l in range(L)]
        tile_gathered = [sem(f"tile_gathered{l}") for l in range(L)]
        tile_added = sem("tile_added")
        tile_step = sem("tile_step")
        block_loaded = sem("block_loaded")
        block_step = sem("block_step")
        block_stored = sem("block_stored")
        passed = sem("passed")

        block = ctx.enter_context(nc.Block())

        def node_table(l):
            return x if l == 0 else hidden

        def uses(l, turn):
            return l * TURNS + turn + 1

        def row_uses(l, turn, slot, short):
            extra = 1 if slot == (G - 1) % RING else 0
            return uses(l, turn) + l * extra + (extra if short else 0)

        TILE_STEPS = ("dst_float", "raw", "score", "spread_score", "spread_dst", "lay_out", "other_pen",
                      "same", "masked", "tile_peak", "new_peak", "lowered", "old_lowered", "repeats",
                      "alpha", "old_scale", "weigh", "add_up", "new_sums", "keep_peak", "is_repeat",
                      "dump_gap", "row_float", "row_int")
        BLOCK_STEPS = ("total", "inverse", "mean", "turn", "mean_turned", "window_turned", "product",
                       "relu", "stats", "aggregate", "log", "inv_std", "normalise")

        def tile_before(name, c):
            return len(TILE_STEPS) * (c - 1) + TILE_STEPS.index(name)

        def block_before(name, c):
            return len(BLOCK_STEPS) * (c - 1) + BLOCK_STEPS.index(name)

        def each_tile(eng, l, body):
            with eng.Fori(0, FULL_TILES) as tile:
                body(tile, l * TILES + tile + 1, False)
            if TILES > FULL_TILES:
                body(FULL_TILES, l * TILES + FULL_TILES + 1, True)

        def each_block(eng, l, body):
            with eng.Fori(0, BLOCKS) as blk:
                body(blk, l * BLOCKS + blk + 1)

        def by_path(eng, grouped, anything):
            eng.wait_ge(general_ready, 1)
            chosen = eng.value_load(general[0:1, 0:1], min_val=0, max_val=1)
            with eng.If(chosen > 0):
                anything()
            with eng.Else():
                grouped()

        HALF_A = 6
        EARLY = 3
        WARM = 3
        TURN_AT, FEATURES_AT, ROWS_AT, TURNED_AT = 3, 6, 8, 5

        def step_on(slot, turn, k):
            return (slot + k) % RING, turn + (slot + k) // RING

        def turns(eng, body):
            body(0, True, False)
            with eng.Fori(1, TURNS - 1) as turn:
                body(turn, False, False)
            body(TURNS - 1, False, True)

        DVE_ONES, DVE_DST = 8, 10
        DVE_TURNED = 17
        DVE_MASKS = 27
        DVE_ATT = 45
        DVE_ALL = 53

        SELECTORS = [(identity, 0, -1, 1.0), (shift_down, 1, -1, 1.0), (shift_up, -1, -1, 1.0),
                     (last_to_first, -(P - 1), P, 1.0), (from_first, 0, 0, 1.0),
                     (from_last, -(P - 1), 0, 1.0), (minus_first, 0, 0, -1.0)]

        @block.gpsimd
        def _(pool):
            for n, (tile, _, _, _) in enumerate(SELECTORS):
                nc.gpsimd.memset(tile[:], 0.0).then_inc(selectors, 1)
            pool.wait_ge(selectors, len(SELECTORS))
            for tile, first, step, value in SELECTORS:
                nc.gpsimd.affine_select(out=tile[:], in_=tile[:], compare_op=ALU.not_equal, fill=value,
                                        base=first, pattern=[[step, P]],
                                        channel_multiplier=1).then_inc(selectors, 1)
            nc.gpsimd.iota(column[:], [[1, P]], base=0, channel_multiplier=0,
                           allow_small_or_imprecise_dtypes=True).then_inc(selectors, 1)
            nc.gpsimd.iota(partition[:], [[0, 1]], base=0, channel_multiplier=1,
                           allow_small_or_imprecise_dtypes=True).then_inc(selectors, 1)

            def gather(l, slot):
                for part, (t0, t1) in enumerate(PARTS):
                    for t in range(t0, t1):
                        nc.gpsimd.indirect_dma_start(
                            rows[:, slot, t, 0:D], None, node_table(l)[0:N, :],
                            bass.IndirectOffsetOnAxis(ap=src_idx[:, slot, t:t + 1], axis=0),
                        ).then_inc(gathered[slot][part], 16)

            for slot in range(RING):
                pool.wait_ge(idx_loaded[slot], 16)
                gather(0, slot)

            def grouped():
                for l in range(L):
                    if l > 0:
                        pool.wait_ge(stored, 16 * G * l)

                    def body(turn, first, last):
                        for slot in range(RING):
                            if first and l == 0:
                                continue
                            n = l * G + RING * turn + slot + 1
                            pool.wait_ge(summed_up, n - RING)
                            pool.wait_ge(idx_loaded[slot], 16 * uses(l, turn))
                            pool.sem_inc(passed, 1)
                            gather(l, slot)

                    turns(pool, body)

            def anything():
                for slot in range(RING):
                    for part, (t0, t1) in enumerate(PARTS):
                        pool.wait_ge(gathered[slot][part], 16 * (t1 - t0))
                for l in range(L):
                    if l > 0:
                        pool.wait_ge(block_stored, 16 * BLOCKS * l)
                    pool.wait_ge(emptied, 16 * (BLOCKS + 1) * (l + 1))
                    table = node_table(l)[0:DUMP, :]

                    def body(tile, c, short):
                        pool.wait_ge(tile_loaded[l], 48 * (tile + 1))
                        pool.sem_inc(passed, 1)
                        for to, what, index in ((rows[:, 0, 0, 0:D], table, tile_src),
                                                (rows[:, 0, 0, C_HOT:C_ROW], table, tile_dst),
                                                (old_sums[:], node_sums, tile_dst)):
                            nc.gpsimd.indirect_dma_start(
                                to, None, what, bass.IndirectOffsetOnAxis(ap=index[:, 0:1], axis=0),
                            ).then_inc(tile_gathered[l], 16)
                        pool.wait_ge(tile_step, len(TILE_STEPS) * c)
                        pool.sem_inc(passed, 1)
                        nc.gpsimd.indirect_dma_start(
                            node_sums, bass.IndirectOffsetOnAxis(ap=sums_row[:, 0:1], axis=0),
                            new_sums[:], None).then_inc(tile_added, 16)

                    each_tile(pool, l, body)

            by_path(pool, grouped, anything)

        SELECTED = 2 * len(SELECTORS) + 2
        NW = 16 * 4

        @block.sync
        def _(sp):
            def load_edges(l, g, slot, n, short):
                sp.dma_start(src_idx[:, slot, :],
                             src[bass.ds(g, 1)].rearrange("o p t -> (o p) t")).then_inc(idx_loaded[slot], 16)
                if not short:
                    sp.dma_start(rows[:, slot, :, D:2 * D],
                                 edge_attr[bass.ds(g * GROUP, GROUP), :]
                                 .rearrange("(p t) d -> p t d", t=K)).then_inc(rows_loaded[slot], 16)
                    return
                left = E - g * GROUP
                full = left // K
                sp.dma_start(rows[0:full, slot, :, D:2 * D],
                             edge_attr[g * GROUP:g * GROUP + full * K, :]
                             .rearrange("(p t) d -> p t d", t=K)).then_inc(rows_loaded[slot], 16)
                sp.dma_start(rows[full:full + 1, slot, 0:left - full * K, D:2 * D],
                             edge_attr[g * GROUP + full * K:E, :]
                             .rearrange("(p t) d -> p t d", p=1)).then_inc(rows_loaded[slot], 16)

            sp.dma_start(dst_int[:], dst).then_inc(dst_loaded, 16)
            for slot in range(RING):
                load_edges(0, slot, slot, slot + 1, False)
            sp.dma_start(w_sb[:], weights.rearrange("l k n -> k l n")).then_inc(weights_loaded, 16)
            sp.dma_start(wr_sb[:], rel_weights.rearrange("l k n -> k l n")).then_inc(weights_loaded, 16)
            sp.dma_start(loop_sb[:], loop_weights.rearrange("l k n -> k l n")).then_inc(weights_loaded, 16)
            sp.dma_start(att_sb[:], att).then_inc(weights_loaded, 16)
            sp.wait_ge(dve_made, DVE_MASKS)
            sp.dma_start(row_masks, masks_t[:].rearrange("g m p -> g (m p)")).then_inc(masks_stored, 16)
            sp.wait_ge(masks_stored, 16)

            def grouped():
                def store(l, g, slot, n):
                    b = slot % 2
                    at = sp.value_load(base_int[0:1, bass.ds(g, 1)] if not isinstance(g, int)
                                       else base_int[0:1, g:g + 1], min_val=0, max_val=N)
                    sp.wait_ge(result_made, n)
                    sp.sem_inc(passed, 1)
                    if not (isinstance(n, int) and n == 1):
                        sp.wait_ge(stored, 16 * (n - 1))
                    sp.sem_inc(passed, 1)
                    to = out if l == L - 1 else hidden
                    sp.dma_start(to[bass.ds(at, P), :], result[b][:]).then_inc(stored, 16)

                def load_masks(g, slot):
                    sp.dma_start(mask_row[0:1, slot, :],
                                 row_masks[bass.ds(g, 1), :]).then_inc(mask_loaded[slot], 16)

                def load_window(l, g, slot, n):
                    at = sp.value_load(base_int[0:1, bass.ds(g, 1)] if not isinstance(g, int)
                                       else base_int[0:1, g:g + 1], min_val=0, max_val=N)
                    sp.dma_start(window[:, slot, :],
                                 node_table(l)[bass.ds(at, P), :]).then_inc(window_loaded[slot], 16)
                    if not (isinstance(g, int) and g < RING):
                        store(l, g - RING, slot, n - RING)
                    if l == L - 1:
                        sp.dma_start(residual[:, slot, :], x[bass.ds(at, P), :]).then_inc(residual_loaded[slot], 16)

                for l in range(L):
                    def body(turn, first, last):
                        for slot in range(RING):
                            g = RING * turn + slot
                            n = l * G + g + 1
                            if not first:
                                sp.wait_ge(summed_up, n - RING)
                                sp.sem_inc(passed, 1)
                                load_edges(l, g, slot, n, last and slot == RING - 1)
                            elif l > 0:
                                sp.wait_ge(summed_up, n - RING)
                                load_edges(l, g, slot, n, False)
                                load_masks(g, slot)
                                store(l - 1, G - RING + slot, slot, n - RING)
                                continue
                            load_masks(g, slot)
                            load_window(l, g, slot, n)
                        if first and l > 0:
                            sp.wait_ge(stored, 16 * G * l)
                            for slot in range(RING):
                                load_window(l, slot, slot, l * G + slot + 1)

                    turns(sp, body)
                for slot in range(RING):
                    store(L - 1, G - RING + slot, slot, L * G - RING + slot + 1)
                sp.wait_ge(stored, 16 * G * L)

            def anything():
                for slot in range(RING):
                    sp.wait_ge(rows_loaded[slot], 16)
                    for part, (t0, t1) in enumerate(PARTS):
                        sp.wait_ge(gathered[slot][part], 16 * (t1 - t0))
                flat = src.rearrange("g p (t o) -> (g p t) o", o=1)
                for l in range(L):
                    if l > 0:
                        sp.wait_ge(block_stored, 16 * BLOCKS * l)
                    with sp.Fori(0, BLOCKS + 1) as blk:
                        sp.dma_start(node_sums[bass.ds(blk * P, P), :], empty_sums[:]).then_inc(emptied, 16)

                    def load(tile, c, short):
                        wide_rows = E - FULL_TILES * P if short else P
                        sp.dma_start(tile_src[:], flat[bass.ds(tile * P, P), :]).then_inc(tile_loaded[l], 16)
                        sp.dma_start(tile_dst[:], dst_flat[bass.ds(tile * P, P), :]).then_inc(tile_loaded[l], 16)
                        sp.dma_start(rows[0:wide_rows, 0, 0, D:2 * D],
                                     edge_attr[bass.ds(tile * P, wide_rows), :]).then_inc(tile_loaded[l], 16)
                        sp.wait_ge(tile_added, 16 * c)
                        sp.sem_inc(passed, 1)

                    each_tile(sp, l, load)

                    def block_pass(blk, c):
                        at = bass.ds(blk * P, P)
                        sp.dma_start(old_sums[:], node_sums[at, :]).then_inc(block_loaded, 16)
                        sp.dma_start(window[:, 0, :], node_table(l)[at, :]).then_inc(block_loaded, 16)
                        sp.dma_start(residual[:, 0, :], x[at, :]).then_inc(block_loaded, 16)
                        sp.wait_ge(block_step, len(BLOCK_STEPS) * c)
                        sp.sem_inc(passed, 1)
                        to = out if l == L - 1 else hidden
                        sp.dma_start(to[at, :], result[0][:]).then_inc(block_stored, 16)
                        sp.wait_ge(block_stored, 16 * c)
                        sp.sem_inc(passed, 1)

                    each_block(sp, l, block_pass)

            by_path(sp, grouped, anything)

        @block.vector
        def _(dve):
            made = [0]

            def step(ins):
                made[0] += 1
                ins.then_inc(dve_made, 1)
                dve.wait_ge(dve_made, made[0])

            V = nc.vector
            step(V.memset(ones[:], 1.0))
            step(V.memset(eps[:], EPS))
            step(V.memset(rows[:, :, :, C_ONE:C_ONE + 1], 1.0))
            step(V.memset(carry_m[0][:], 0.0))
            step(V.memset(carry_m[1][:], 0.0))
            step(V.memset(last_before[:], -1.0))
            step(V.memset(faults[:], 0.0))
            step(V.memset(carry_pen[:], -BIG))
            assert made[0] == DVE_ONES
            dve.wait_ge(dst_loaded, 16)
            step(V.tensor_copy(dst_f[:], dst_int[:]))
            step(V.tensor_copy(last_before[:, 1:G], dst_f[:, 0:G - 1, K - 1]))
            assert made[0] == DVE_DST
            dve.wait_ge(pe_made, 1)
            step(V.tensor_copy(base[:], ps_row[:, 0:G]))
            step(V.tensor_copy(base_int[:], base[0:1, :]))
            step(V.tensor_tensor(rel[:], dst_f[:], base[:].unsqueeze(2).broadcast_to([P, G, K]), ALU.subtract))
            step(V.tensor_tensor(base_step[:, 1:G], base[:, 1:G], base[:, 0:G - 1], ALU.subtract))
            step(V.tensor_copy(firsts_t[:], ps_out[0:G, 0:P]))
            step(V.tensor_copy(lasts_t[:], ps_out[0:G, P:2 * P]))
            step(V.tensor_copy(before_t[:], ps_out[0:G, 2 * P:3 * P]))
            assert made[0] == DVE_TURNED
            step(V.memset(masks_t[:], -BIG))
            step(V.tensor_tensor(spans_t[:], firsts_t[:], lasts_t[:], ALU.not_equal))
            step(V.tensor_scalar(spans_t[:], spans_t[:], -BIG, None, ALU.mult))
            step(V.tensor_tensor(masks_t[:, 0, 1:P], lasts_t[:, 0:P - 1], firsts_t[:, 1:P], ALU.not_equal))
            step(V.tensor_tensor(masks_t[:, 0, 0:1], before_t[:, P - 1:P], firsts_t[:, 0:1], ALU.not_equal))
            step(V.tensor_scalar(masks_t[:, 0, :], masks_t[:, 0, :], -BIG, None, ALU.mult))
            step(V.tensor_tensor(masks_t[:, 1, 1:P], masks_t[:, 0, 1:P], spans_t[:, 0:P - 1], ALU.add))
            step(V.tensor_copy(masks_t[:, 2, 0:P - 1], masks_t[:, 0, 1:P]))
            step(V.tensor_tensor(masks_t[:, 3, 0:P - 1], masks_t[:, 2, 0:P - 1], spans_t[:, 1:P], ALU.add))
            step(V.memset(step_pen[:], 0.0))
            assert made[0] == DVE_MASKS
            step(V.tensor_tensor(step_pen[:, :, 1:K], dst_f[:, :, 1:K], dst_f[:, :, 0:K - 1], ALU.not_equal))
            step(V.tensor_scalar(step_pen[:], step_pen[:], -BIG, None, ALU.mult))
            step(V.tensor_copy(back_pen[:], step_pen[:, :, K:0:-1]))
            step(V.tensor_tensor(head_pen[:], dst_f[:], dst_f[:, :, 0:1].broadcast_to([P, G, K]), ALU.not_equal))
            step(V.tensor_scalar(head_pen[:], head_pen[:], -BIG, None, ALU.mult))
            step(V.tensor_tensor(tail_pen[:], dst_f[:], dst_f[:, :, K - 1:K].broadcast_to([P, G, K]),
                                 ALU.not_equal))
            step(V.tensor_scalar(tail_pen[:], tail_pen[:], -BIG, None, ALU.mult))
            dve.wait_ge(selectors, SELECTED)
            step(V.tensor_scalar(carry_pen[:, 1:G], base_step[:, 1:G], partition[:, 0:1], -BIG,
                                 ALU.not_equal, ALU.mult))
            step(V.tensor_tensor(unsorted[:, :, 0:K - 1], dst_f[:, :, 0:K - 1], dst_f[:, :, 1:K], ALU.is_gt))
            step(V.tensor_reduce(faults[:, 0:1], unsorted[:, :, 0:K - 1], AX.XY, ALU.max))
            step(V.tensor_tensor(spans_t[:, 0:P - 1], lasts_t[:, 0:P - 1], firsts_t[:, 1:P], ALU.is_gt))
            step(V.tensor_tensor(spans_t[:, P - 1:P], before_t[:, P - 1:P], firsts_t[:, 0:1], ALU.is_gt))
            step(V.tensor_reduce(faults[0:G, 1:2], spans_t[:], AX.X, ALU.max))
            step(V.tensor_scalar(base_step[:, 0:1], base[:, G - 1:G], -1.0, float(N - 1), ALU.mult, ALU.add))
            step(V.tensor_scalar(wide[:], base_step[:], float(P - 1), None, ALU.is_gt))
            step(V.tensor_reduce(faults[:, 2:3], wide[:], AX.X, ALU.max))
            step(V.tensor_scalar(faults[:, 3:4], base[:, 0:1], 0.0, None, ALU.is_gt))
            dve.wait_ge(weights_loaded, NW)
            for l in range(L):
                for c in range(3):
                    ins = V.tensor_scalar(att_wide[:, l, c, :], ones[:], att_sb[:, 3 * l + c:3 * l + c + 1],
                                          None, ALU.mult)
            step(ins)
            assert made[0] == DVE_ATT
            dve.wait_ge(pe_made, 2)
            step(V.tensor_copy(w_turned[:], ps_turn[:, 0:L * D].rearrange("p (l d) -> p l d", l=L)))
            step(V.tensor_copy(wr_turned[:], ps_turn[:, L * D:2 * L * D].rearrange("p (l d) -> p l d", l=L)))
            dve.wait_ge(pe_made, 3)
            for l in range(L):
                V.tensor_copy(w_loop[:, l, :], ps_sum[l][:, 0:D])
                V.memset(ps_score[l][:, C_ONE:C_ONE + 1], 0.0)
                ins = V.tensor_scalar(dst_wide[:, l, :], ones[:], ps_out[:, l:l + 1], None, ALU.mult)
            step(ins)
            step(V.tensor_reduce(fault_row[:], ps_col[0:1, 0:4], AX.X, ALU.max))
            step(V.tensor_scalar(fault_row[:], fault_row[:], 1.0, None, ALU.min))
            step(V.tensor_scalar(below[:], column[:], partition[:, 0:1], None, ALU.is_lt))
            step(V.memset(empty_sums[:], 0.0))
            step(V.memset(empty_sums[:, C_HOT:C_HOT + 1], -BIG))
            V.tensor_copy(general[:], fault_row[:]).then_inc(general_ready, 1)
            assert made[0] == DVE_ALL, made[0]

            def grouped():
                def hots(slot, turn, tiles):
                    for t in tiles:
                        g = RING * turn + slot
                        at = rel[:, bass.ds(g, 1), t:t + 1].rearrange("p o t -> p (o t)")
                        ins = V.tensor_scalar(rows[:, slot, t, C_HOT:C_ROW], column[:], at, None, ALU.is_equal)
                    ins.then_inc(hot_made, 1)

                def score_group(l, turn, slot, short, after_part, before_row):
                    g = RING * turn + slot
                    n = l * G + g + 1
                    b = slot % 2
                    next_slot, next_turn = step_on(slot, turn, 1)
                    dve.wait_ge(hot_made, 2 * n)
                    dve.wait_ge(rows_loaded[slot], 16 * row_uses(l, turn, slot, short))
                    dve.wait_ge(dst_scored, n)
                    for part, (t0, t1) in enumerate(PARTS):
                        dve.wait_ge(gathered[slot][part], 16 * (t1 - t0) * uses(l, turn))
                        for t in range(t0, t1):
                            ins = V.tensor_tensor_reduce(products[:, t, :], rows[:, slot, t, 0:C_ROW],
                                                         ps_score[b][:, 0:C_ROW], 1.0, 0.0, ALU.mult,
                                                         ALU.add, score_raw[:, b, t:t + 1])
                        if part == 0:
                            after_part()
                    ins.then_inc(raw_made, 1)
                    dve.wait_ge(raw_made, n)
                    V.scalar_tensor_tensor(score[:, b, :], score_raw[:, b, :], NEG_SLOPE,
                                           score_raw[:, b, :], ALU.mult, ALU.max).then_inc(score_made, 1)
                    dve.wait_ge(score_made, n)
                    fwd_pen = step_pen[:, bass.ds(g, 1), 0:K].rearrange("p o t -> p (o t)")
                    bwd_pen = back_pen[:, bass.ds(g, 1), :].rearrange("p o t -> p (o t)")
                    V.tensor_tensor_scan(run_fwd[:, b, :], fwd_pen, score[:, b, :], -BIG, ALU.add, ALU.max)
                    V.tensor_tensor_scan(run_bwd[:, b, ::-1], bwd_pen, score[:, b, ::-1], -BIG,
                                         ALU.add, ALU.max).then_inc(runs_made, 1)
                    if not short:
                        if not (l == 0 and isinstance(g, int) and g + 1 < RING):
                            dve.wait_ge(summed_up, n + 1 - RING)
                        hots(next_slot, next_turn, range(HALF_A))
                    before_row()
                    dve.wait_ge(row_ready, n)
                    V.tensor_tensor_scan(carried[0:1, b, 0:P], mask_row[0:1, slot, P:2 * P],
                                         ps_row[0:1, 0:P], -BIG, ALU.add, ALU.max)
                    V.tensor_tensor_scan(carried[0:1, b, 2 * P - 1:P - 1:-1],
                                         mask_row[0:1, slot, 4 * P - 1:3 * P - 1:-1],
                                         ps_col[0:1, 2 * P - 1:P - 1:-1], -BIG,
                                         ALU.add, ALU.max).then_inc(carried_made, 1)
                    if not short:
                        hots(next_slot, next_turn, range(HALF_A, K))
                    dve.wait_ge(runs_made, n)
                    V.tensor_tensor(peak_a[:, b, :], run_fwd[:, b, :], run_bwd[:, b, :],
                                    ALU.max).then_inc(peak_a_made, 1)
                    dve.wait_ge(peak_a_made, n)
                    dve.wait_ge(col_ready, n)
                    head = head_pen[:, bass.ds(g, 1), :].rearrange("p o t -> p (o t)")
                    tail = tail_pen[:, bass.ds(g, 1), :].rearrange("p o t -> p (o t)")
                    V.scalar_tensor_tensor(peak_b[:, b, :], head, ps_col[:, 0:1], peak_a[:, b, :],
                                           ALU.add, ALU.max).then_inc(peak_b_made, 1)
                    dve.wait_ge(peak_b_made, n)
                    V.scalar_tensor_tensor(peak[:, b, :], tail, ps_col[:, 1:2], peak_b[:, b, :],
                                           ALU.add, ALU.max).then_inc(peak_made, 1)
                    dve.wait_ge(peak_made, n)
                    V.tensor_tensor(lowered[:, b, :], score[:, b, :], peak[:, b, :],
                                    ALU.subtract).then_inc(lowered_made, 1)

                def carried_drop(n, b):
                    dve.wait_ge(drop_ready, n)
                    V.tensor_scalar(drop[:, b:b + 1], ps_col[:, 2:3], 0.0, None,
                                    ALU.min).then_inc(drop_made, 1)

                def inverse_total(n, b):
                    dve.wait_ge(summed_up, n)
                    V.tensor_scalar(total[:, b:b + 1], ps_sum[b][:, C_ONE:C_ONE + 1], TINY, None,
                                    ALU.max).then_inc(total_made, 1)
                    dve.wait_ge(total_made, n)
                    V.reciprocal(inv_total[:, b:b + 1], total[:, b:b + 1]).then_inc(inv_total_made, 1)

                def residual_sum(l, turn, slot):
                    b = slot % 2
                    m = RING * turn + slot + 1
                    dve.wait_ge(out_ready, l * G + m)
                    dve.wait_ge(residual_loaded[slot], 16 * (turn + 1))
                    V.scalar_tensor_tensor(summed[b][:], ps_out[:, 0:D], 0.0, residual[:, slot, :],
                                           ALU.max, ALU.add).then_inc(summed_made, 1)
                    dve.wait_ge(summed_made, m)
                    V.bn_stats(stats[:, b, :], summed[b][:]).then_inc(stats_made, 1)
                    dve.wait_ge(stats_made, m)
                    dve.sem_inc(passed, 1)
                    V.bn_aggr(mean_var[:, b, :], stats[:, b, :]).then_inc(mean_var_made, 1)

                def normalise(l, turn, slot):
                    b = slot % 2
                    m = RING * turn + slot + 1
                    dve.wait_ge(inv_std_made, m)
                    if not (isinstance(m, int) and m <= 2):
                        dve.wait_ge(stored, 16 * (l * G + m - 2))
                    V.tensor_scalar(result[b][:], summed[b][:], mean_var[:, b, 0:1], inv_std[:, b:b + 1],
                                    ALU.subtract, ALU.mult).then_inc(result_made, 1)

                def nothing():
                    pass

                for l in range(L):
                    if l > 0:
                        dve.wait_ge(summed_up, l * G - RING + 1)
                    hots(0, 0, range(HALF_A))
                    hots(0, 0, range(HALF_A, K))
                    score_group(l, 0, 0, False, nothing, nothing)

                    def body(turn, first, last):
                        for slot in range(RING):
                            n = l * G + RING * turn + slot + 1
                            has_before = not (first and slot == 0)
                            before = step_on(slot, turn, -1)
                            if has_before:
                                inverse_total(n - 1, 1 - slot % 2)
                            late = has_before and l == L - 1
                            if not (last and slot == RING - 1):
                                after, after_turn = step_on(slot, turn, 1)
                                score_group(l, after_turn, after, last and slot == RING - 2,
                                            lambda: carried_drop(n, slot % 2),
                                            (lambda: residual_sum(l, before[1], before[0])) if late else nothing)
                            else:
                                carried_drop(n, slot % 2)
                                if late:
                                    residual_sum(l, before[1], before[0])
                            if late:
                                normalise(l, before[1], before[0])

                    turns(dve, body)
                    inverse_total((l + 1) * G, (G - 1) % 2)
                    if l == L - 1:
                        residual_sum(l, TURNS - 1, RING - 1)
                        normalise(l, TURNS - 1, RING - 1)

            def anything():
                col = {n: tile_work[:, i:i + 1] for i, n in enumerate(
                    ("raw", "score", "tile_peak", "new_peak", "lowered", "old_lowered", "repeats",
                     "alpha", "old_scale", "is_repeat", "dump_gap", "row_float"))}

                for l in range(L):
                    dve.wait_ge(score_ready, l + 1)

                    def tile_pass(tile, c, short):
                        dve.wait_ge(tile_loaded[l], 48 * (tile + 1))
                        V.tensor_copy(tile_dst_f[:], tile_dst[:]).then_inc(tile_step, 1)
                        dve.wait_ge(tile_gathered[l], 48 * (tile + 1))
                        dve.wait_ge(tile_step, tile_before("raw", c))
                        V.tensor_tensor_reduce(products[:, 0, :], rows[:, 0, 0, 0:C_ROW], ps_score[0][:, 0:C_ROW],
                                               1.0, 0.0, ALU.mult, ALU.add, col["raw"]).then_inc(tile_step, 1)
                        dve.wait_ge(tile_step, tile_before("score", c))
                        V.scalar_tensor_tensor(col["score"], col["raw"], NEG_SLOPE, col["raw"],
                                               ALU.mult, ALU.max).then_inc(tile_step, 1)
                        dve.wait_ge(tile_step, tile_before("spread_score", c))
                        V.tensor_scalar(spread[:, 0, :], ones[:], col["score"], None,
                                        ALU.mult).then_inc(tile_step, 1)
                        dve.wait_ge(tile_step, tile_before("spread_dst", c))
                        V.tensor_scalar(spread[:, 1, :], ones[:], tile_dst_f[:], None,
                                        ALU.mult).then_inc(tile_step, 1)
                        dve.wait_ge(tile_step, tile_before("other_pen", c))
                        V.tensor_scalar(other_pen[:], ps_row[:, P:2 * P], tile_dst_f[:], -BIG,
                                        ALU.not_equal, ALU.mult).then_inc(tile_step, 1)
                        dve.wait_ge(tile_step, tile_before("same", c))
                        V.tensor_scalar(same[:], ps_row[:, P:2 * P], tile_dst_f[:], None,
                                        ALU.is_equal).then_inc(tile_step, 1)
                        dve.wait_ge(tile_step, tile_before("masked", c))
                        V.tensor_tensor(masked[:], other_pen[:], ps_row[:, 0:P], ALU.add).then_inc(tile_step, 1)
                        dve.wait_ge(tile_step, tile_before("tile_peak", c))
                        V.tensor_reduce(col["tile_peak"], masked[:], AX.X, ALU.max).then_inc(tile_step, 1)
                        dve.wait_ge(tile_step, tile_before("new_peak", c))
                        V.tensor_tensor(col["new_peak"], col["tile_peak"], old_sums[:, C_HOT:C_HOT + 1],
                                        ALU.max).then_inc(tile_step, 1)
                        dve.wait_ge(tile_step, tile_before("lowered", c))
                        V.tensor_tensor(col["lowered"], col["score"], col["new_peak"],
                                        ALU.subtract).then_inc(tile_step, 1)
                        dve.wait_ge(tile_step, tile_before("old_lowered", c))
                        V.tensor_tensor(col["old_lowered"], old_sums[:, C_HOT:C_HOT + 1], col["new_peak"],
                                        ALU.subtract).then_inc(tile_step, 1)
                        dve.wait_ge(tile_step, tile_before("repeats", c))
                        V.tensor_tensor_reduce(products[:, 1, 0:P], same[:], below[:], 1.0, 0.0,
                                               ALU.mult, ALU.add, col["repeats"]).then_inc(tile_step, 1)
                        dve.wait_ge(tile_step, tile_before("new_sums", c))
                        V.scalar_tensor_tensor(new_sums[:, 0:C_HOT], old_sums[:, 0:C_HOT], col["old_scale"],
                                               ps_sum[0][:, 0:C_HOT], ALU.mult, ALU.add).then_inc(tile_step, 1)
                        dve.wait_ge(tile_step, tile_before("keep_peak", c))
                        V.tensor_copy(new_sums[:, C_HOT:C_HOT + 1], col["new_peak"]).then_inc(tile_step, 1)
                        dve.wait_ge(tile_step, tile_before("is_repeat", c))
                        V.tensor_scalar(col["is_repeat"], col["repeats"], 0.5, None,
                                        ALU.is_gt).then_inc(tile_step, 1)
                        dve.wait_ge(tile_step, tile_before("dump_gap", c))
                        V.scalar_tensor_tensor(col["dump_gap"], partition[:], float(DUMP), tile_dst_f[:],
                                               ALU.add, ALU.subtract).then_inc(tile_step, 1)
                        dve.wait_ge(tile_step, tile_before("row_float", c))
                        V.scalar_tensor_tensor(col["row_float"], col["dump_gap"], col["is_repeat"],
                                               tile_dst_f[:], ALU.mult, ALU.add).then_inc(tile_step, 1)
                        dve.wait_ge(tile_step, tile_before("row_int", c))
                        V.tensor_copy(sums_row[:], col["row_float"]).then_inc(tile_step, 1)

                    each_tile(dve, l, tile_pass)

                    def block_pass(blk, c):
                        dve.wait_ge(block_loaded, 48 * c)
                        V.tensor_scalar(total[:, 0:1], old_sums[:, C_ONE:C_ONE + 1], TINY, None,
                                        ALU.max).then_inc(block_step, 1)
                        dve.wait_ge(block_step, block_before("inverse", c))
                        V.reciprocal(inv_total[:, 0:1], total[:, 0:1]).then_inc(block_step, 1)
                        if l < L - 1:
                            dve.wait_ge(block_step, block_before("relu", c))
                            V.tensor_scalar(result[0][:], ps_out[:, 0:D], 0.0, None, ALU.max).then_inc(
                                block_step, BLOCK_STEPS.index("normalise") - BLOCK_STEPS.index("relu") + 1)
                            return
                        dve.wait_ge(block_step, block_before("relu", c))
                        V.scalar_tensor_tensor(summed[0][:], ps_out[:, 0:D], 0.0, residual[:, 0, :],
                                               ALU.max, ALU.add).then_inc(block_step, 1)
                        dve.wait_ge(block_step, block_before("stats", c))
                        V.bn_stats(stats[:, 0, :], summed[0][:]).then_inc(block_step, 1)
                        dve.wait_ge(block_step, block_before("aggregate", c))
                        dve.sem_inc(passed, 1)
                        V.bn_aggr(mean_var[:, 0, :], stats[:, 0, :]).then_inc(block_step, 1)
                        dve.wait_ge(block_step, block_before("normalise", c))
                        V.tensor_scalar(result[0][:], summed[0][:], mean_var[:, 0, 0:1], inv_std[:, 0:1],
                                        ALU.subtract, ALU.mult).then_inc(block_step, 1)

                    each_block(dve, l, block_pass)

            by_path(dve, grouped, anything)

        @block.tensor
        def _(pe):
            T = nc.tensor
            pe.wait_ge(selectors, SELECTED)
            pe.wait_ge(dve_made, DVE_DST)
            T.matmul(ps_row[:, 0:G], from_first[:], dst_f[:, :, 0], start=True, stop=True)
            T.transpose(ps_out[0:G, 0:P], dst_f[:, :, 0], identity[:])
            T.transpose(ps_out[0:G, P:2 * P], dst_f[:, :, K - 1], identity[:])
            T.transpose(ps_out[0:G, 2 * P:3 * P], last_before[:], identity[:]).then_inc(pe_made, 1)
            pe.wait_ge(weights_loaded, NW)
            for l in range(L):
                T.transpose(ps_turn[:, l * D:(l + 1) * D], w_sb[:, l, :], identity[:])
            for l in range(L):
                ins = T.transpose(ps_turn[:, (L + l) * D:(L + l + 1) * D], wr_sb[:, l, :], identity[:])
            ins.then_inc(pe_made, 1)
            pe.wait_ge(dve_made, DVE_ATT + 2)
            for l in range(L):
                T.matmul(ps_sum[l][:, 0:D], w_turned[:, l, :], loop_sb[:, l, :], start=True, stop=True)
                T.matmul(ps_out[:, l:l + 1], w_turned[:, l, :], att_sb[:, 3 * l + 1:3 * l + 2], start=True, stop=True)
            T.matmul(ps_col[0:1, 0:4], ones[:, 0:1], faults[:], start=True, stop=True).then_inc(pe_made, 1)
            pe.wait_ge(dve_made, DVE_ALL)

            def score_vectors(l):
                for b in range(2):
                    T.matmul(ps_score[b][:, 0:D], att_wide[:, l, 0, :], w_turned[:, l, :], start=True, stop=True)
                    T.matmul(ps_score[b][:, D:2 * D], att_wide[:, l, 2, :], wr_turned[:, l, :],
                             start=True, stop=True)

            def grouped():
                def turn_window(l, turn, slot):
                    pe.wait_ge(window_loaded[slot], 16 * uses(l, turn))
                    T.transpose(ps_turn[:, 2 * D:3 * D], window[:, slot, :], identity[:]).then_inc(window_turned, 1)

                def score_window(l, slot, n):
                    pe.wait_ge(window_t_made, n)
                    T.matmul(ps_score[slot % 2][:, C_HOT:C_ROW], dst_wide[:, l, :], window_t[:, slot, :],
                             start=True, stop=True).then_inc(dst_scored, 1)

                def turn_means(n):
                    pe.wait_ge(mean_made, n)
                    for h in range(2):
                        ins = T.transpose(ps_turn[:, h * D:(h + 1) * D], mean_rows[:, h * D:(h + 1) * D],
                                          identity[:])
                    ins.then_inc(mean_turned, 1)

                def next_features(l, slot, n):
                    pe.wait_ge(mean_t_made, n)
                    T.matmul(ps_out[:, 0:D], window_t[:, slot, :], w_loop[:, l, :], start=True, stop=False)
                    T.matmul(ps_out[:, 0:D], mean_t[:, 0:D], w_sb[:, l, :], start=False, stop=False)
                    T.matmul(ps_out[:, 0:D], mean_t[:, D:2 * D], wr_sb[:, l, :],
                             start=False, stop=True).then_inc(out_ready, 1)

                def lay_rows(l, turn, slot, n, start):
                    b = slot % 2
                    pe.wait_ge(mask_loaded[slot], 16 * uses(l, turn))
                    if not start:
                        pe.wait_ge(drop_made, n - 1)
                        T.matmul(ps_row[0:1, 0:P], peak[:, 1 - b, K - 1:K], last_to_first[:],
                                 start=True, stop=False)
                    T.matmul(ps_row[0:1, 0:P], ones[0:1, 0:1], mask_row[0:1, slot, 0:P],
                             start=start, stop=False)
                    T.matmul(ps_col[0:1, P:2 * P], ones[0:1, 0:1], mask_row[0:1, slot, 2 * P:3 * P],
                             start=True, stop=False)
                    pe.wait_ge(runs_made, n)
                    T.matmul(ps_row[0:1, 0:P], run_fwd[:, b, K - 1:K], shift_down[:], start=False, stop=True)
                    T.matmul(ps_col[0:1, P:2 * P], run_bwd[:, b, 0:1], shift_up[:],
                             start=False, stop=True).then_inc(row_ready, 1)

                def back_to_columns(slot, n):
                    b = slot % 2
                    pe.wait_ge(carried_made, n)
                    for c in range(2):
                        ins = T.matmul(ps_col[:, c:c + 1], carried[0:1, b, c * P:(c + 1) * P],
                                       ones[0:1, 0:1], start=True, stop=True)
                    ins.then_inc(col_ready, 1)

                def peak_rise(slot, n, start):
                    b = slot % 2
                    pe.wait_ge(peak_made, n)
                    if not start:
                        T.matmul(ps_col[:, 2:3], from_last[:], peak[:, 1 - b, K - 1:K], start=True, stop=False)
                    T.matmul(ps_col[:, 2:3], minus_first[:], peak[:, b, 0:1],
                             start=start, stop=True).then_inc(drop_ready, 1)

                def add_edges(slot, n, tiles, alone=False):
                    b = slot % 2
                    for t in tiles:
                        pe.wait_ge(weighted_made, K * (n - 1) + t + 1)
                        ins = T.matmul(ps_sum[b][:, 0:C_HOT], weighted[:, b, t, :],
                                       rows[:, slot, t, 0:C_HOT], start=t == 0,
                                       stop=alone and t == K - 1)
                    return ins

                def add_carried(slot, n):
                    b = slot % 2
                    pe.wait_ge(carry_made, n)
                    pe.wait_ge(sums_made, n - 1)
                    return T.matmul(ps_sum[b][:, 0:C_HOT], carry_m[b][:], sums[1 - b][:],
                                    start=False, stop=True)

                def keep_warm(products):
                    for _ in range(products):
                        T.matmul(ps_row[:, 2 * P:4 * P], identity[:], w_sb[:, 0:2, :], start=True, stop=True)

                for l in range(L):
                    n = l * G + 1
                    score_vectors(l)
                    turn_window(l, 0, 0)
                    score_window(l, 0, n)
                    turn_window(l, 0, 1)
                    lay_rows(l, 0, 0, n, True)
                    back_to_columns(0, n)
                    peak_rise(0, n, True)
                    score_window(l, 1, n + 1)

                    def body(turn, first, last):
                        for slot in range(RING):
                            n = l * G + RING * turn + slot + 1
                            has_before = not (first and slot == 0)
                            has_after = not (last and slot == RING - 1)
                            has_window = not (last and slot >= RING - 2)
                            after, after_turn = step_on(slot, turn, 1)
                            window_slot, window_turn = step_on(slot, turn, 2)
                            before = step_on(slot, turn, -1)[0]
                            add_edges(slot, n, range(0, TURN_AT))
                            if has_before:
                                turn_means(n - 1)
                            add_edges(slot, n, range(TURN_AT, FEATURES_AT))
                            if has_before:
                                next_features(l, before, n - 1)
                            rows_at = K - 1 if last and slot == RING - 2 else ROWS_AT
                            add_edges(slot, n, range(FEATURES_AT, rows_at))
                            if has_after:
                                lay_rows(l, after_turn, after, n + 1, False)
                            ins = add_edges(slot, n, range(rows_at, K), not has_before)
                            if has_before:
                                ins = add_carried(slot, n)
                            ins.then_inc(summed_up, 1)
                            if has_after:
                                back_to_columns(after, n + 1)
                            if has_window:
                                turn_window(l, window_turn, window_slot)
                            if has_after:
                                peak_rise(after, n + 1, False)
                            if has_window:
                                score_window(l, window_slot, n + 2)
                            if not (last and slot >= RING - 2):
                                keep_warm(WARM)

                    turns(pe, body)
                    turn_means((l + 1) * G)
                    next_features(l, RING - 1, (l + 1) * G)

            def anything():
                for l in range(L):
                    if l > 0:
                        pe.wait_ge(block_step, len(BLOCK_STEPS) * BLOCKS * l)
                    score_vectors(l)
                    T.matmul(ps_score[0][:, C_HOT:C_ROW], att_wide[:, l, 1, :], w_turned[:, l, :],
                             start=True, stop=True).then_inc(score_ready, 1)

                    def tile_pass(tile, c, short):
                        pe.wait_ge(tile_step, tile_before("lay_out", c))
                        T.matmul(ps_row[:, 0:P], spread[:, 0, :], identity[:], start=True, stop=True)
                        T.matmul(ps_row[:, P:2 * P], spread[:, 1, :], identity[:],
                                 start=True, stop=True).then_inc(tile_step, 1)
                        pe.wait_ge(tile_step, tile_before("add_up", c))
                        T.matmul(ps_sum[0][:, 0:C_HOT], same[:], tile_rows[:],
                                 start=True, stop=True).then_inc(tile_step, 1)

                    each_tile(pe, l, tile_pass)

                    def block_pass(blk, c):
                        pe.wait_ge(block_step, block_before("turn", c))
                        for h in range(2):
                            T.transpose(ps_turn[:, h * D:(h + 1) * D], mean_rows[:, h * D:(h + 1) * D],
                                        identity[:])
                        T.transpose(ps_turn[:, 2 * D:3 * D], window[:, 0, :], identity[:]).then_inc(block_step, 1)
                        pe.wait_ge(block_step, block_before("product", c))
                        T.matmul(ps_out[:, 0:D], window_t[:, 0, :], w_loop[:, l, :], start=True, stop=False)
                        T.matmul(ps_out[:, 0:D], mean_t[:, 0:D], w_sb[:, l, :], start=False, stop=False)
                        T.matmul(ps_out[:, 0:D], mean_t[:, D:2 * D], wr_sb[:, l, :],
                                 start=False, stop=True).then_inc(block_step, 1)

                    each_block(pe, l, block_pass)

            by_path(pe, grouped, anything)

        @block.scalar
        def _(act):
            A = nc.scalar
            act.wait_ge(dve_made, DVE_ALL)
            nc.scalar.preload_act_table_set("natural_log_exp_and_others")

            def grouped():
                def window_copy(slot, n):
                    act.wait_ge(window_turned, n)
                    A.activation(window_t[:, slot, :], ps_turn[:, 2 * D:3 * D],
                                 ACT.Copy).then_inc(window_t_made, 1)

                def averages(n, b):
                    act.wait_ge(inv_total_made, n)
                    A.activation(mean_rows[:], ps_sum[b][:, 0:2 * D], ACT.Copy,
                                 scale=inv_total[:, b:b + 1]).then_inc(mean_made, 1)
                    A.activation(sums[b][:], ps_sum[b][:, 0:C_HOT], ACT.Copy).then_inc(sums_made, 1)

                def averages_turned(n):
                    act.wait_ge(mean_turned, n)
                    A.activation(mean_t[:], ps_turn[:, 0:2 * D], ACT.Copy).then_inc(mean_t_made, 1)

                def output(l, n, b):
                    if l < L - 1:
                        act.wait_ge(out_ready, n)
                        if not (isinstance(n, int) and n <= 2):
                            act.wait_ge(stored, 16 * (n - 2))
                        A.activation(result[b][:], ps_out[:, 0:D], ACT.Relu).then_inc(result_made, 1)
                    else:
                        m = n - l * G
                        act.wait_ge(mean_var_made, m)
                        A.activation(log_var[:, b:b + 1], mean_var[:, b, 1:2], ACT.Ln,
                                     bias=eps[:]).then_inc(log_var_made, 1)
                        act.wait_ge(log_var_made, m)
                        A.activation(inv_std[:, b:b + 1], log_var[:, b:b + 1], ACT.Exp,
                                     scale=-0.5).then_inc(inv_std_made, 1)

                def weigh(slot, n, tiles):
                    b = slot % 2
                    act.wait_ge(alpha_made, n)
                    for t in tiles:
                        A.activation(weighted[:, b, t, :], rows[:, slot, t, C_HOT:C_ROW], ACT.Copy,
                                     scale=alpha[:, b, t:t + 1]).then_inc(weighted_made, 1)

                def exps(slot, n):
                    b = slot % 2
                    act.wait_ge(lowered_made, n)
                    A.activation(alpha[:, b, :], lowered[:, b, :], ACT.Exp).then_inc(alpha_made, 1)
                    weigh(slot, n, range(0, EARLY))

                def carried_weight(g, n, b):
                    act.wait_ge(drop_made, n)
                    A.activation(carry_m[b][:, 0:1], drop[:, b:b + 1], ACT.Exp,
                                 bias=carry_pen[:, bass.ds(g, 1)]).then_inc(carry_made, 1)

                for l in range(L):
                    n = l * G + 1
                    window_copy(0, n)
                    window_copy(1, n + 1)
                    exps(0, n)

                    def body(turn, first, last):
                        for slot in range(RING):
                            g = RING * turn + slot
                            n = l * G + g + 1
                            has_before = not (first and slot == 0)
                            if has_before:
                                averages(n - 1, 1 - slot % 2)
                            weigh(slot, n, range(EARLY, TURNED_AT))
                            if has_before:
                                averages_turned(n - 1)
                            weigh(slot, n, range(TURNED_AT, K))
                            carried_weight(g, n, slot % 2)
                            if has_before:
                                output(l, n - 1, 1 - slot % 2)
                            if not (last and slot >= RING - 2):
                                window_copy((slot + 2) % RING, n + 2)
                            if not (last and slot == RING - 1):
                                exps((slot + 1) % RING, n + 1)

                    turns(act, body)
                    averages((l + 1) * G, (G - 1) % 2)
                    averages_turned((l + 1) * G)
                    output(l, (l + 1) * G, (G - 1) % 2)

            def anything():
                alpha_col, old_scale = tile_work[:, 7:8], tile_work[:, 8:9]
                for l in range(L):
                    def tile_pass(tile, c, short):
                        act.wait_ge(tile_step, tile_before("alpha", c))
                        A.activation(alpha_col, tile_work[:, 4:5], ACT.Exp).then_inc(tile_step, 1)
                        act.wait_ge(tile_step, tile_before("old_scale", c))
                        A.activation(old_scale, tile_work[:, 5:6], ACT.Exp).then_inc(tile_step, 1)
                        act.wait_ge(tile_step, tile_before("weigh", c))
                        A.activation(tile_rows[:], rows[:, 0, 0, 0:C_HOT], ACT.Copy,
                                     scale=alpha_col).then_inc(tile_step, 1)

                    each_tile(act, l, tile_pass)

                    def block_pass(blk, c):
                        act.wait_ge(block_step, block_before("mean", c))
                        A.activation(mean_rows[:], old_sums[:, 0:2 * D], ACT.Copy,
                                     scale=inv_total[:, 0:1]).then_inc(block_step, 1)
                        act.wait_ge(block_step, block_before("mean_turned", c))
                        A.activation(mean_t[:], ps_turn[:, 0:2 * D], ACT.Copy).then_inc(block_step, 1)
                        act.wait_ge(block_step, block_before("window_turned", c))
                        A.activation(window_t[:, 0, :], ps_turn[:, 2 * D:3 * D], ACT.Copy).then_inc(block_step, 1)
                        if l == L - 1:
                            act.wait_ge(block_step, block_before("log", c))
                            A.activation(log_var[:, 0:1], mean_var[:, 0, 1:2], ACT.Ln,
                                         bias=eps[:]).then_inc(block_step, 1)
                            act.wait_ge(block_step, block_before("inv_std", c))
                            A.activation(inv_std[:, 0:1], log_var[:, 0:1], ACT.Exp,
                                         scale=-0.5).then_inc(block_step, 1)

                    each_block(act, l, block_pass)

            by_path(act, grouped, anything)


_IN = ("x", "src", "dst", "edge_attr_128", "L0_gnn_W", "L0_gnn_Wr", "L0_gnn_Att", "L0_gnn_Loop")


def kernel(**inputs):
    import numpy as np
    import concourse.bacc as bacc
    from concourse.bass_utils import run_bass_kernel_spmd

    x, src, dst, edge_attr, w, wr, att, loop = (np.asarray(inputs[n]) for n in _IN)
    nodes, edges, layers = x.shape[0], src.shape[0], w.shape[0]
    tiles = -(-edges // P)
    groups = -(-tiles // (K * RING)) * RING
    padded = groups * K * P
    src_pad = np.pad(src, (0, padded - edges)).reshape(groups, P, K)
    dst_pad = np.pad(dst, (0, padded - edges), constant_values=nodes).reshape(groups, P, K)
    arrays = {
        "x": np.pad(x, ((0, P), (0, 0))),
        "src": src_pad,
        "dst": np.ascontiguousarray(dst_pad.transpose(1, 0, 2)),
        "dst_flat": dst_pad.reshape(padded, 1),
        "edge_attr": edge_attr,
        "weights": w,
        "rel_weights": wr,
        "att": np.ascontiguousarray(att.reshape(layers, 3, D).transpose(2, 0, 1).reshape(D, layers * 3)),
        "loop_weights": loop,
    }
    nc = bacc.Bacc("TRN2", target_bir_lowering=False, num_devices=1)
    args = [nc.dram_tensor(n, a.shape, mybir.dt.from_np(a.dtype), kind="ExternalInput").ap()
            for n, a in arrays.items()]
    out = nc.dram_tensor("out", (nodes + P, D), F32, kind="ExternalOutput").ap()
    gnn_program(nc, *args, out, {"nodes": nodes, "edges": edges, "groups": groups, "layers": layers})
    r = run_bass_kernel_spmd(nc, [arrays], core_ids=[0])
    return r.results[0]["out"][:nodes]
```
